# Optimizing a Trainium2 kernel written in Bass

```python
import numpy as np
import jax
import jax.numpy as jnp

def _softmax(x, axis=-1):
    return jax.nn.softmax(x, axis=axis)

def _gelu(x):
    return jax.nn.gelu(x, approximate=True)

def _silu(x):
    return jax.nn.silu(x)

def _sigmoid(x):
    return jax.nn.sigmoid(x)

def _layernorm(x, axis=-1, eps=1e-05):
    m = jnp.mean(x, axis=axis, keepdims=True)
    v = jnp.var(x, axis=axis, keepdims=True)
    return (x - m) / jnp.sqrt(v + eps)

def _scatter_add(tgt, idx, src, axis=0):
    return tgt.at[idx].add(src)

def _segment_sum(src, seg, n):
    return jax.ops.segment_sum(src, seg, n)
kernel_name = 'mk_gnn_resnorm_d1_gnn_r64_e32840'

def setup_inputs(seed: int=0):
    np.random.seed(seed)
    _w = jnp.asarray

    def _rec_inputs():
        import jax
        import jax.numpy as jnp
        _gk = jax.random.key(seed)
        x = -0.000202 + 1 * jax.random.normal(jax.random.fold_in(_gk, 1), (100000, 128), jnp.float32)
        src = jax.random.randint(jax.random.fold_in(_gk, 2), (25000,), 0, 100000, jnp.int32)
        dst = jax.random.randint(jax.random.fold_in(_gk, 3), (25000,), 0, 100000, jnp.int32)
        _o = jnp.argsort(dst, stable=True)
        src = src[_o]
        dst = dst[_o]
        edge_attr_64 = -9.77346e-05 + 0.999888 * jax.random.normal(jax.random.fold_in(_gk, 11), (25000, 64), jnp.float32)
        edge_weight1 = jax.random.uniform(jax.random.fold_in(_gk, 13), (25000, 1), jnp.float32, 0.0, 0.999998)
        node_vec1 = jax.random.uniform(jax.random.fold_in(_gk, 14), (100000, 1), jnp.float32, 0.0, 0.999884)
        return (x, src, dst, edge_attr_64, edge_weight1, node_vec1)
    x, src, dst, edge_attr_64, edge_weight1, node_vec1 = _rec_inputs()

    def _L0_gnn_setup():
        import jax, jax.numpy as jnp
        import numpy as np
        N_NODES, N_EDGES = (50000, 12500)
        NODE_DIM, EDGE_DIM, HIDDEN, HEADS = (128, 64, 128, 8)
        HEAD_DIM = HIDDEN // HEADS
        key = jax.random.key(seed)
        ks = jax.random.split(key, 24)

        def lin(k, fan_in, fan_out):
            lim = 1.0 / np.sqrt(fan_in)
            kw, kb = jax.random.split(k)
            W = jax.random.uniform(kw, (fan_in, fan_out), jnp.float32, -lim, lim)
            b = jax.random.uniform(kb, (fan_out,), jnp.float32, -lim, lim)
            return (W, b)
        inp = {}
        inp['nodes'] = jax.random.normal(ks[0], (N_NODES, NODE_DIM), jnp.float32)
        inp['edges'] = jax.random.normal(ks[1], (N_EDGES, EDGE_DIM), jnp.float32)
        inp['edge_index'] = jax.random.randint(ks[2], (2, N_EDGES), 0, N_NODES, jnp.int32)
        inp['conservation_scores'] = jax.random.uniform(ks[3], (N_NODES, 1), jnp.float32)
        inp['distances'] = jax.random.uniform(ks[4], (N_EDGES, 1), jnp.float32)
        inp['Wq'], inp['bq'] = lin(ks[5], NODE_DIM, HIDDEN)
        inp['Wk'], inp['bk'] = lin(ks[6], NODE_DIM, HIDDEN)
        inp['Wv'], inp['bv'] = lin(ks[7], NODE_DIM, HIDDEN)
        inp['We'], inp['be'] = lin(ks[8], EDGE_DIM, HEADS)
        inp['Wc1'], inp['bc1'] = lin(ks[9], 1, 32)
        inp['Wc2'], inp['bc2'] = lin(ks[10], 32, HEADS)
        inp['Wd1'], inp['bd1'] = lin(ks[11], 1, 16)
        inp['Wd2'], inp['bd2'] = lin(ks[12], 16, HEADS)
        inp['Wo'], inp['bo'] = lin(ks[13], HIDDEN, NODE_DIM)
        inp['gamma'] = jnp.ones((NODE_DIM,), jnp.float32)
        inp['beta'] = jnp.zeros((NODE_DIM,), jnp.float32)
        return inp
    _L0_gnn_all = _L0_gnn_setup()
    _L0_gnn_in = {k: v for k, v in _L0_gnn_all.items() if k in ('Wq', 'bq', 'Wk', 'bk', 'Wv', 'bv', 'We', 'be', 'Wc1', 'bc1', 'Wc2', 'bc2', 'Wd1', 'bd1', 'Wd2', 'bd2', 'Wo', 'bo', 'gamma', 'beta')}
    del _L0_gnn_all
    return {'x': x, 'src': src, 'dst': dst, 'edge_attr_64': edge_attr_64, 'edge_weight1': edge_weight1, 'node_vec1': node_vec1, 'L0_gnn_Wq': _L0_gnn_in['Wq'], 'L0_gnn_bq': _L0_gnn_in['bq'], 'L0_gnn_Wk': _L0_gnn_in['Wk'], 'L0_gnn_bk': _L0_gnn_in['bk'], 'L0_gnn_Wv': _L0_gnn_in['Wv'], 'L0_gnn_bv': _L0_gnn_in['bv'], 'L0_gnn_We': _L0_gnn_in['We'], 'L0_gnn_be': _L0_gnn_in['be'], 'L0_gnn_Wc1': _L0_gnn_in['Wc1'], 'L0_gnn_bc1': _L0_gnn_in['bc1'], 'L0_gnn_Wc2': _L0_gnn_in['Wc2'], 'L0_gnn_bc2': _L0_gnn_in['bc2'], 'L0_gnn_Wd1': _L0_gnn_in['Wd1'], 'L0_gnn_bd1': _L0_gnn_in['bd1'], 'L0_gnn_Wd2': _L0_gnn_in['Wd2'], 'L0_gnn_bd2': _L0_gnn_in['bd2'], 'L0_gnn_Wo': _L0_gnn_in['Wo'], 'L0_gnn_bo': _L0_gnn_in['bo'], 'L0_gnn_gamma': _L0_gnn_in['gamma'], 'L0_gnn_beta': _L0_gnn_in['beta']}

def reference(x, src, dst, edge_attr_64, edge_weight1, node_vec1, L0_gnn_Wq, L0_gnn_bq, L0_gnn_Wk, L0_gnn_bk, L0_gnn_Wv, L0_gnn_bv, L0_gnn_We, L0_gnn_be, L0_gnn_Wc1, L0_gnn_bc1, L0_gnn_Wc2, L0_gnn_bc2, L0_gnn_Wd1, L0_gnn_bd1, L0_gnn_Wd2, L0_gnn_bd2, L0_gnn_Wo, L0_gnn_bo, L0_gnn_gamma, L0_gnn_beta):
    import jax
    import jax.numpy as jnp

    def _L0_gnn_ref(nodes, edges, edge_index, conservation_scores, distances, Wq, bq, Wk, bk, Wv, bv, We, be, Wc1, bc1, Wc2, bc2, Wd1, bd1, Wd2, bd2, Wo, bo, gamma, beta):
        import jax, jax.numpy as jnp
        import numpy as np
        N_NODES, N_EDGES = (50000, 12500)
        NODE_DIM, EDGE_DIM, HIDDEN, HEADS = (128, 64, 128, 8)
        HEAD_DIM = HIDDEN // HEADS
        N = nodes.shape[0]
        src, tgt = (edge_index[0], edge_index[1])
        q = (nodes @ Wq + bq).reshape(N, HEADS, HEAD_DIM)
        k = (nodes @ Wk + bk).reshape(N, HEADS, HEAD_DIM)
        v = (nodes @ Wv + bv).reshape(N, HEADS, HEAD_DIM)
        scores = jnp.einsum('ehd,ehd->eh', q[src], k[tgt]) / np.sqrt(HEAD_DIM)
        scores = scores + edges @ We + be
        cons = jax.nn.sigmoid(jax.nn.relu(conservation_scores @ Wc1 + bc1) @ Wc2 + bc2)
        scores = scores * cons[tgt]
        scores = scores + jax.nn.relu(distances @ Wd1 + bd1) @ Wd2 + bd2
        seg_max = jax.ops.segment_max(scores, tgt, num_segments=N)
        w = jnp.exp(scores - seg_max[tgt])
        seg_sum = jax.ops.segment_sum(w, tgt, num_segments=N)
        weights = w / seg_sum[tgt]
        attended = weights[..., None] * v[tgt]
        agg = jax.ops.segment_sum(attended, tgt, num_segments=N).reshape(N, HIDDEN)
        out = agg @ Wo + bo
        x = nodes + out
        mu = jnp.mean(x, axis=-1, keepdims=True)
        var = jnp.var(x, axis=-1, keepdims=True)
        return (x - mu) / jnp.sqrt(var + 1e-05) * gamma + beta
    edge_index = jnp.stack([src, dst])
    x = _layernorm(x + _L0_gnn_ref(x, edge_attr_64, edge_index, node_vec1, edge_weight1, L0_gnn_Wq, L0_gnn_bq, L0_gnn_Wk, L0_gnn_bk, L0_gnn_Wv, L0_gnn_bv, L0_gnn_We, L0_gnn_be, L0_gnn_Wc1, L0_gnn_bc1, L0_gnn_Wc2, L0_gnn_bc2, L0_gnn_Wd1, L0_gnn_bd1, L0_gnn_Wd2, L0_gnn_bd2, L0_gnn_Wo, L0_gnn_bo, L0_gnn_gamma, L0_gnn_beta), axis=-1)
    return x

_drawn_inputs = setup_inputs


def setup_inputs(seed=0):
    import zlib

    import numpy as np

    out = dict(_drawn_inputs(seed))
    spreads = {'L0_gnn_gamma': (1.0, 0.2), 'L0_gnn_beta': (0.0, 0.1)}
    factors = {'edge_attr_64': 64.0,
     'edge_weight1': 64.0,
     'node_vec1': 64.0,
     'L0_gnn_Wq': 64.0,
     'L0_gnn_bq': 64.0,
     'L0_gnn_Wk': 64.0,
     'L0_gnn_bk': 64.0,
     'L0_gnn_bv': 8.0,
     'L0_gnn_We': 64.0,
     'L0_gnn_be': 64.0,
     'L0_gnn_Wc1': 64.0,
     'L0_gnn_bc1': 64.0,
     'L0_gnn_Wc2': 64.0,
     'L0_gnn_bc2': 64.0,
     'L0_gnn_Wd1': 64.0,
     'L0_gnn_bd1': 64.0,
     'L0_gnn_Wd2': 64.0,
     'L0_gnn_bd2': 64.0}
    for name, (base, spread) in spreads.items():
        noise = np.random.default_rng([zlib.crc32(name.encode()), seed]).standard_normal(out[name].shape)
        drawn = base * np.exp(spread * noise) if base else spread * noise
        out[name] = jnp.asarray(drawn.astype(out[name].dtype))
    for name, factor in factors.items():
        out[name] = (out[name] * factor).astype(out[name].dtype)
    return out
```

```python
from contextlib import ExitStack

import concourse.bass as bass
from concourse import mybir

F32 = mybir.dt.float32
BF16 = mybir.dt.bfloat16
I32 = mybir.dt.int32
ALU = mybir.AluOpType
ACT = mybir.ActivationFunctionType
AX = mybir.AxisListType

P = 128
N_NODES = 100000
D = 128
E_DIM = 64
HEADS = 8
HEAD_DIM = D // HEADS
CONS_H = 32
DIST_H = 16
N_EDGES = 25000
TILES = -(-N_EDGES // P)
PAD_EDGES = P * TILES
G = 4
GROUPS = TILES // G
GE = G * P
XN = D + 1
ROWS = 8
CW = ROWS * D
CHUNK = P * ROWS
FULL_CHUNKS = N_NODES // CHUNK
REST_P = (N_NODES - FULL_CHUNKS * CHUNK) // ROWS
CHUNKS = FULL_CHUNKS + 1
UNROLL = 4
PEELED = 2
EPS = 1e-5
BIG = 3e38
NO_ROW = 131072.0
assert TILES % G == 0 and REST_P * ROWS + FULL_CHUNKS * CHUNK == N_NODES
assert CHUNKS == 2 * GROUPS and GROUPS == 12 * UNROLL + 1 and E_DIM * 2 == P


def after(engine, sem, count):
    if not isinstance(count, int) or count > 0:
        engine.wait_ge(sem, count)


class Memory:
    pass


def gnn_kernel(nc, a, out):
    ctx = ExitStack()
    with ctx:
        m = Memory()

        def sb(name, shape, dt=F32):
            return ctx.enter_context(nc.sbuf_tensor(name, shape, dt))

        def sem(name):
            return ctx.enter_context(nc.semaphore(name))

        ident = sb("ident", [P, P])
        eps = sb("eps", [P, 1])
        ones = sb("ones", [P, P])
        ones_bf = sb("ones_bf", [P, P], BF16)
        Wq = sb("Wq", [P, D])
        Wk = sb("Wk", [P, D])
        Wv = sb("Wv", [P, D])
        Wo = sb("Wo", [P, D])
        bq = sb("bq", [P, 1])
        bk = sb("bk", [P, 1])
        bv = sb("bv", [P, 1])
        bo = sb("bo", [P, 1])
        beta = sb("beta", [P, 1])
        head_sel3 = sb("head_sel3", [P, 3 * HEADS])
        head_sel = head_sel3[:, HEADS:2 * HEADS]
        We2 = sb("We2", [P, 2 * HEADS])
        Wc1s = sb("Wc1s", [G, G * CONS_H])
        Wd1s = sb("Wd1s", [G, G * DIST_H])
        Wc2s = sb("Wc2s", [G * CONS_H, G * HEADS])
        Wd2s = sb("Wd2s", [G * DIST_H, G * HEADS])
        bc1 = sb("bc1", [G * CONS_H, 1])
        bd1 = sb("bd1", [G * DIST_H, 1])
        be_b = sb("be_b", [P, HEADS])
        bc2_b = sb("bc2_b", [P, HEADS])
        bd2_b = sb("bd2_b", [P, HEADS])
        gamma_b = sb("gamma_b", [P, D])
        bo_b = sb("bo_b", [P, D])
        beta_b = sb("beta_b", [P, D])
        beta_rows = sb("beta_rows", [P, G * D], BF16)
        src_i = sb("src_i", [P, TILES], I32)
        dst_i = sb("dst_i", [P, TILES], I32)
        dist = sb("dist", [P, TILES])
        dst_f = sb("dst_f", [P, TILES])
        unsorted_p = sb("unsorted_p", [P, 1])
        unsorted_i = sb("unsorted_i", [P, 1], I32)
        same = sb("same", [P, TILES])
        cont = sb("cont", [P, HEADS * TILES + 1])
        in_first = sb("in_first", [P, TILES])
        in_last = sb("in_last", [P, TILES])
        neg_first = sb("neg_first", [P, TILES])
        neg_last = sb("neg_last", [P, TILES])
        link8 = sb("link8", [P, 2, HEADS])
        link_r = sb("link_r", [HEADS, 2, P])
        mul_r = sb("mul_r", [HEADS, 4, P])
        neg_r = sb("neg_r", [HEADS, 4, P])
        edge_r = sb("edge_r", [HEADS, 2, P])
        carry_r = sb("carry_r", [HEADS, 2, P])
        carry = sb("carry", [P, 2, HEADS])
        rep_f = sb("rep_f", [P, TILES])
        scat_f = sb("scat_f", [P, TILES])
        scat_i = sb("scat_i", [P, TILES], I32)
        x_in = sb("x_in", [P, UNROLL, CW])
        y = sb("y", [P, UNROLL, CW])
        o = sb("o", [P, 2, CW])
        st1 = sb("st1", [P, 2, ROWS, 6])
        st2 = sb("st2", [P, 2, ROWS, 6])
        tmp1 = sb("tmp1", [P, 2, 5, ROWS])
        tmp2 = sb("tmp2", [P, 2, 5, ROWS])
        norm1 = sb("norm1", [P, 2, 2, ROWS])
        norm2 = sb("norm2", [P, 2, 2, ROWS])
        xs = sb("xs", [P, 2, G, D])
        xd = sb("xd", [P, 2, G, XN])
        idx = sb("idx", [P, 2, 2, G], I32)
        dist_s = sb("dist_s", [P, 2, G])
        ea = sb("ea", [P, 2, G * E_DIM])
        xsT = sb("xsT", [P, GE])
        xdT = sb("xdT", [P, TILES * P])
        eaT = sb("eaT", [P, 2 * P])
        cdT = sb("cdT", [G, 2 * P])
        qT = sb("qT", [P, GE])
        prod = sb("prod", [P, GE])
        h1 = sb("h1", [G * CONS_H, P])
        h2 = sb("h2", [G * DIST_H, P])
        cons_all = sb("cons_all", [P, HEADS, TILES])
        dist_all = sb("dist_all", [P, HEADS, TILES])
        scores = sb("scores", [P, HEADS, TILES])
        scat_stage = sb("scat_stage", [P, UNROLL, G], I32)

        x_flat = x_in[:, :, :].rearrange("p a b -> p (a b)")
        y_flat = y[:, :, :].rearrange("p a b -> p (a b)")
        o_flat = o[:, :, :].rearrange("p a b -> p (a b)")
        HT = HEADS * TILES
        cont_f = cont[:, 0:HT]
        cont_b = cont[:, 1:HT + 1]
        early = xdT[:, TILES * P - 2048:TILES * P]
        part_f = early[:, 0:2 * D].rearrange("p (s d) -> p s d", s=2)
        part_bf = early[:, 2 * D:4 * D].bitcast(BF16)[:, 0:3 * D] \
            .rearrange("p (s d) -> p s d", s=3)
        prev_f = early[:, 4 * D:4 * D + TILES]
        prev_i = early[:, 4 * D + 2 * TILES:4 * D + 3 * TILES].bitcast(I32)
        unsorted_t = early[:, 4 * D + TILES:4 * D + 2 * TILES]

        def heads(ap):
            return ap.rearrange("p (h t) -> p h t", h=HEADS)

        run = x_flat[:, 0:HT]
        ends = x_flat[:, HT:2 * HT]
        total = y_flat[:, 0:HT]
        neg_f = y_flat[:, HT:2 * HT]
        all_row = y_flat[:, HT:2 * HT]
        all_prod = o_flat[:, 0:HT]
        all_dst = x_flat[:, 2 * HT:2 * HT + TILES]
        all_mask = x_flat[:, 2 * HT + TILES:2 * HT + 2 * TILES]
        all_idx = x_flat[:, 2 * HT + 2 * TILES:2 * HT + 3 * TILES]
        all_less = x_flat[:, 2 * HT + 3 * TILES:2 * HT + 4 * TILES]
        edge_no = o_flat[:, HT:HT + TILES]
        all_count = y_flat[:, 2 * HT:2 * HT + TILES]
        all_col = y_flat[:, 2 * HT + TILES:2 * HT + TILES + 2 + HEADS]
        sx, aggT, yT, xbT = (x_flat[:, 2 * n * GE:2 * (n + 1) * GE].rearrange("p (s n) -> p s n", s=2)
                             for n in range(4))
        u = y_flat[:, 2 * GE:4 * GE].rearrange("p (s n) -> p s n", s=2)
        vT = y_flat[:, 6 * GE:8 * GE].rearrange("p (s n) -> p s n", s=2)
        rows_out = o_flat.rearrange("p (s n) -> p s n", s=UNROLL)

        scr_rows = nc.dram_tensor("scr_rows", [P, HEADS + 2, TILES], F32).ap()

        banks = [ctx.enter_context(nc.psum_tensor(f"bank{i}", [P, 2, 512], F32)) for i in range(4)]
        z_ps = [banks[0][:, :, :], banks[1][:, :, :]]
        bank_xs = banks[2][:, 0, :]
        bank_xd = banks[2][:, 1, :]
        bank_ea = banks[3][:, 0, :]
        bank_sc = banks[3][:, 1, :]
        S_ps, V_ps = banks[0][:, 0, :], banks[0][:, 1, :]
        YT_ps = [banks[1][:, s, :] for s in range(2)]
        Y_ps = [banks[2][:, s, :] for s in range(2)]
        Z_ps = [banks[3][:, s, :] for s in range(2)]

        zeroed = sem("zeroed")
        ident_made = sem("ident_made")
        idx_loaded = sem("idx_loaded")
        consts_loaded = sem("consts_loaded")
        masks_made = sem("masks_made")
        links_turned = sem("links_turned")
        beta_split = sem("beta_split")
        masks_made_pe = sem("masks_made_pe")
        setup_step = sem("setup_step")
        x_loaded = [sem(f"x_loaded{j}") for j in range(UNROLL)]
        y_ready = sem("y_ready")
        stat1 = sem("stat1")
        var1_ready = sem("var1_ready")
        std1_ready = sem("std1_ready")
        inv1_ready = sem("inv1_ready")
        var2_ready = sem("var2_ready")
        std2_ready = sem("std2_ready")
        inv2_ready = sem("inv2_ready")
        norm1_ready = sem("norm1_ready")
        u_ready = sem("u_ready")
        ug_ready = sem("ug_ready")
        z_ready = sem("z_ready")
        stat2 = sem("stat2")
        norm2_ready = sem("norm2_ready")
        out_ready = sem("out_ready")
        out_stored = [sem(f"out_stored{j}") for j in range(2)]
        idx_staged = sem("idx_staged")
        dist_staged = sem("dist_staged")
        gathered = [sem(f"gathered{j}") for j in range(2)]
        ea_loaded = [sem(f"ea_loaded{j}") for j in range(2)]
        turned = sem("turned")
        turned_kept = sem("turned_kept")
        qk_ready = sem("qk_ready")
        hidden_ps = sem("hidden_ps")
        q_kept = sem("q_kept")
        hidden_kept = sem("hidden_kept")
        prod_ready = sem("prod_ready")
        parts_ps = sem("parts_ps")
        sig_ready = sem("sig_ready")
        scores_ready = sem("scores_ready")
        soft_step = sem("soft_step")
        edges_out = sem("edges_out")
        edges_turned = sem("edges_turned")
        carries_out = sem("carries_out")
        carries_turned = sem("carries_turned")
        fast_done = sem("fast_done")
        reduced = sem("reduced")
        shifted = sem("shifted")
        exp_ready = sem("exp_ready")
        all_dma = sem("all_dma")
        all_step = sem("all_step")
        all_fence = sem("all_fence")
        
        S_ready = sem("S_ready")
        sx_ready = sem("sx_ready")
        v_ready = sem("v_ready")
        v_kept = sem("v_kept")
        agg_ready = sem("agg_ready")
        yT_ps = sem("yT_ps")
        yT_ready = sem("yT_ready")
        xb_ready = sem("xb_ready")
        y2_ready = sem("y2_ready")
        norm3_ready = sem("norm3_ready")
        u2_ready = sem("u2_ready")
        ug2_ready = sem("ug2_ready")
        z2_ready = sem("z2_ready")
        norm4_ready = sem("norm4_ready")
        rows_ready = sem("rows_ready")
        scat_staged = sem("scat_staged")
        scattered = [sem(f"scattered{j}") for j in range(UNROLL)]

        def width(i):
            return REST_P if isinstance(i, int) and i == CHUNKS - 1 else P

        def chunk_rows(t, i):
            w = width(i)
            return t[bass.ds(i * CHUNK, w * ROWS), :].rearrange("(p r) d -> p (r d)", r=ROWS)

        def x_free(i):
            return i - UNROLL + 1

        def steps(engine, step, last, whole, peeled=PEELED):
            for i in range(peeled * UNROLL):
                step(i, i // UNROLL, i % UNROLL)
            with engine.Fori(peeled, whole) as k:
                for j in range(UNROLL):
                    step(k * UNROLL + j, k, j)
            for i in range(whole * UNROLL, last):
                step(i, i // UNROLL, i % UNROLL)

        def there(i, n):
            return not isinstance(i, int) or 0 <= i < n

        def half(k, j):
            return k * (UNROLL // 2) + j // 2

        ea_v = a["edge_attr"].rearrange("(p t) f -> p (t f)", t=TILES)

        block = ctx.enter_context(nc.Block())

        @block.sync
        def _(sp):
            flat = a["dst"]
            sp.dma_start(src_i[:, :], a["src"].rearrange("(p t) -> p t", t=TILES)).then_inc(idx_loaded, 16)
            sp.dma_start(dst_i[:, :], flat.rearrange("(p t) -> p t", t=TILES)).then_inc(idx_loaded, 16)
            sp.wait_ge(zeroed, 1)
            sp.dma_start(prev_i[1:P, :], flat[TILES - 1:P * TILES - 1].rearrange("(p t) -> p t", t=TILES))\
              .then_inc(idx_loaded, 16)
            sp.dma_start(prev_i[0:1, 1:TILES], flat[0:TILES - 1].rearrange("(p t) -> p t", p=1))\
              .then_inc(idx_loaded, 16)
            sp.dma_start(dist[:, :], a["edge_weight"].rearrange("(p t) -> p t", t=TILES)).then_inc(idx_loaded, 16)

            def load_x(i, k, j):
                after(sp, z_ready, x_free(i))
                w = width(i)
                sp.dma_start(x_in[0:w, j, :], chunk_rows(a["x"], i)).then_inc(x_loaded[j], 16)

            def load_ea(g, s):
                after(sp, turned, g - 1)
                sp.dma_start(ea[:, s, :], ea_v[:, bass.ds(g * (G * E_DIM), G * E_DIM)]).then_inc(ea_loaded[s], 16)

            load_x(0, 0, 0)
            load_ea(0, 0)
            load_x(1, 0, 1)

            def step(i, k, j):
                g = half(k, j)
                if there(i + 2, CHUNKS):
                    load_x(i + 2, k if j < 2 else k + 1, (j + 2) % UNROLL)
                if j % 2 == 0 and there(g + 1, GROUPS):
                    load_ea(g + 1, (j // 2 + 1) % 2)
                if there(i - 4, CHUNKS):
                    sp.wait_ge(out_ready, i - 3)
                    w = width(i - 4)
                    sp.dma_start(chunk_rows(out, i - 4), o[0:w, j % 2, :]).then_inc(out_stored[j % 2], 16)

            steps(sp, step, CHUNKS + 4, CHUNKS // UNROLL - 1)

        @block.gpsimd
        def _(pool):
            pool.memset(prev_i[0:1, 0:1], -1).then_inc(zeroed, 1)
            for t in (We2, Wc1s, Wd1s, Wc2s, Wd2s):
                last = pool.memset(t[:, :], 0.0)
            last.then_inc(zeroed, 1)
            pool.memset(ident[:, :], 0.0).then_inc(ident_made, 1)
            pool.memset(head_sel3[:, :], 0.0).then_inc(ident_made, 1)
            pool.wait_ge(ident_made, 2)
            pool.memset(head_sel, float(HEAD_DIM) ** -0.5).then_inc(ident_made, 1)
            pool.wait_ge(ident_made, 3)
            pool.affine_select(out=ident[:, :], in_=ident[:, :], compare_op=ALU.not_equal, fill=1.0,
                               base=0, pattern=[[-1, P]], channel_multiplier=1).then_inc(ident_made, 1)
            pool.affine_select(out=head_sel, in_=head_sel, compare_op=ALU.is_ge, fill=0.0,
                               base=0, pattern=[[-HEAD_DIM, HEADS]], channel_multiplier=1).then_inc(ident_made, 1)
            pool.wait_ge(ident_made, 5)
            pool.affine_select(out=head_sel, in_=head_sel, compare_op=ALU.is_ge, fill=0.0,
                               base=HEAD_DIM - 1, pattern=[[HEAD_DIM, HEADS]], channel_multiplier=-1)\
                .then_inc(ident_made, 1)
            pool.memset(ones[:, :], 1.0)
            pool.memset(eps[:, :], EPS)
            pool.memset(ones_bf[:, :], 1.0).then_inc(ident_made, 1)

            def stage(g, s):
                pool.tensor_copy(idx[:, s, 0, :], src_i[:, bass.ds(g * G, G)])
                pool.tensor_copy(idx[:, s, 1, :], dst_i[:, bass.ds(g * G, G)]).then_inc(idx_staged, 1)

            def gather_src(s):
                for t in range(G):
                    pool.indirect_dma_start(xs[:, s, t, :], None, a["x"],
                                            bass.IndirectOffsetOnAxis(ap=idx[:, s, 0, t:t + 1], axis=0))\
                        .then_inc(gathered[s], 16)

            def gather_dst(s):
                for t in range(G):
                    pool.indirect_dma_start(xd[:, s, t, :], None, a["xn"],
                                            bass.IndirectOffsetOnAxis(ap=idx[:, s, 1, t:t + 1], axis=0))\
                        .then_inc(gathered[s], 16)

            def add_bo(i, k, j):
                pool.wait_ge(x_loaded[j], k * 16 + 16)
                w = width(i)
                pool.tensor_tensor(
                    y[0:w, j, :].rearrange("p (r d) -> p r d", d=D),
                    x_in[0:w, j, :].rearrange("p (r d) -> p r d", d=D),
                    bo_b[0:w, None, :].to_broadcast([w, ROWS, D]), ALU.add).then_inc(y_ready, 1)

            pool.wait_ge(idx_loaded, 80)
            stage(0, 0)
            stage(1, 1)
            pool.tensor_copy(dist_s[:, 0, :], dist[:, 0:G]).then_inc(dist_staged, 1)
            pool.wait_ge(idx_staged, 2)
            gather_src(0)
            gather_dst(0)
            pool.wait_ge(consts_loaded, CONST_DMAS * 16)

            def step(i, k, j):
                g = half(k, j)
                s = (j // 2 + 1) % 2
                if j % 2 == 0:
                    if there(g + 1, GROUPS):
                        pool.wait_ge(idx_staged, g + 2)
                        after(pool, turned, g)
                    add_bo(i, k, j)
                    if there(g + 1, GROUPS):
                        pool.tensor_copy(dist_s[:, s, :], dist[:, bass.ds((g + 1) * G, G)]).then_inc(dist_staged, 1)
                        gather_src(s)
                else:
                    if there(g + 2, GROUPS):
                        pool.wait_ge(gathered[1 - s], (k + 1) * (16 * 2 * G))
                    add_bo(i, k, j)
                    if there(g + 2, GROUPS):
                        stage(g + 2, 1 - s)
                    if there(g + 1, GROUPS):
                        gather_dst(s)

            steps(pool, step, CHUNKS, CHUNKS // UNROLL - 1)

            pool.wait_ge(masks_made, 1)
            is_unsorted = pool.value_load(unsorted_i[0:1, 0:1])

            def all_pairs(n, values, into, op, empty, count):
                first = n == 0
                dmas = 48 * n + 48 * P * n
                c = count

                def link(ins, at):
                    ins.then_inc(all_step, 1)
                    pool.wait_ge(all_step, at)
                    pool.sem_inc(all_fence, 1)

                link(pool.memset(into, empty), c + 1)
                link(pool.memset(all_count, 0.0) if first else pool.memset(all_less, 0.0), c + 2)
                link(pool.iota(edge_no, pattern=[[1, TILES]], base=0, channel_multiplier=TILES,
                               allow_small_or_imprecise_dtypes=True) if first else pool.memset(all_less, 0.0), c + 3)
                c += 3
                pool.dma_start(scr_rows[:, 0:HEADS, :], heads(values)).then_inc(all_dma, 16)
                pool.dma_start(scr_rows[:, HEADS, :], dst_f[:, :]).then_inc(all_dma, 16)
                pool.dma_start(scr_rows[:, HEADS + 1, :], edge_no).then_inc(all_dma, 16)
                pool.wait_ge(all_dma, dmas + 48)
                dmas += 48
                steps_of = (8 if op == ALU.max else 4) + (4 if first else 0)
                with pool.Fori(0, P) as q:
                    pool.dma_start(heads(all_row), scr_rows[bass.ds(q, 1), 0:HEADS, :]
                                   .to_broadcast([P, HEADS, TILES])).then_inc(all_dma, 16)
                    pool.dma_start(all_dst, scr_rows[bass.ds(q, 1), HEADS, :].to_broadcast([P, TILES]))\
                        .then_inc(all_dma, 16)
                    pool.dma_start(all_idx, scr_rows[bass.ds(q, 1), HEADS + 1, :].to_broadcast([P, TILES]))\
                        .then_inc(all_dma, 16)
                    pool.wait_ge(all_dma, q * 48 + (dmas + 48))
                    pool.sem_inc(all_fence, 1)
                    with pool.Fori(0, TILES) as t:
                        at = [q * (TILES * steps_of) + t * steps_of + c]

                        def one(ins):
                            at[0] = at[0] + 1
                            link(ins, at[0])

                        one(pool.tensor_copy(all_col[:, 0:1], all_dst[:, bass.ds(t, 1)]))
                        one(pool.tensor_scalar(all_mask, dst_f[:, :], all_col[:, 0:1], None, ALU.is_equal))
                        if first:
                            one(pool.tensor_copy(all_col[:, 1:2], all_idx[:, bass.ds(t, 1)]))
                            one(pool.tensor_scalar(all_less, edge_no, all_col[:, 1:2], None, ALU.is_gt))
                            one(pool.tensor_tensor(all_less, all_less, all_mask, ALU.mult))
                            one(pool.tensor_tensor(all_count, all_count, all_less, ALU.add))
                        mask_b = all_mask[:, None, :].to_broadcast([P, HEADS, TILES])
                        value_b = heads(all_row)[:, :, bass.ds(t, 1)].to_broadcast([P, HEADS, TILES])
                        if op == ALU.max:
                            one(pool.tensor_copy(all_col[:, 2:2 + HEADS], heads(all_row)[:, :, bass.ds(t, 1)]
                                                 .rearrange("p h o -> p (h o)")))
                            for h in range(HEADS):
                                ins = pool.tensor_scalar(heads(all_prod)[:, h, :], heads(into)[:, h, :],
                                                         all_col[:, 2 + h:3 + h], None, ALU.max)
                            one(ins)
                            one(pool.tensor_tensor(heads(all_prod), heads(all_prod), mask_b, ALU.mult))
                            one(pool.tensor_scalar(all_mask, all_mask, -1.0, 1.0, ALU.mult, ALU.add))
                            one(pool.tensor_tensor(heads(into), heads(into), mask_b, ALU.mult))
                        else:
                            one(pool.tensor_tensor(heads(all_prod), mask_b, value_b, ALU.mult))
                        one(pool.tensor_tensor(into, into, all_prod, ALU.add))
                c += P * TILES * steps_of
                if first:
                    link(pool.tensor_scalar(rep_f[:, :], all_count, 0.0, None, ALU.is_equal), c + 1)
                    link(pool.tensor_scalar(scat_f[:, :], dst_f[:, :], NO_ROW, None, ALU.subtract), c + 2)
                    link(pool.tensor_tensor(scat_f[:, :], scat_f[:, :], rep_f[:, :], ALU.mult), c + 3)
                    link(pool.tensor_scalar(scat_f[:, :], scat_f[:, :], NO_ROW, None, ALU.add), c + 4)
                    link(pool.tensor_copy(scat_i[:, :], scat_f[:, :]), c + 5)
                    c += 5
                return c

            c = 0
            for n, (op, empty) in enumerate([(ALU.max, -BIG), (ALU.add, 0.0)]):
                pool.wait_ge(fast_done, n + 1)
                with pool.If(is_unsorted):
                    for s in range(2):
                        pool.wait_ge(out_stored[s], CHUNKS // 2 * 16)
                    c = all_pairs(n, scores[:, :, :].rearrange("p h t -> p (h t)"), total, op, empty, c)
                pool.sem_inc(reduced, 1)

            def stage_scat(g, j):
                pool.tensor_copy(scat_stage[:, j, :], scat_i[:, bass.ds(g * G, G)]).then_inc(scat_staged, 1)

            for s in range(2):
                pool.wait_ge(out_stored[s], CHUNKS // 2 * 16)
            stage_scat(0, 0)

            def scatter(g, k, j):
                pool.wait_ge(scat_staged, g + 1)
                pool.wait_ge(rows_ready, g + 1)
                if there(g + 1, GROUPS):
                    after(pool, scattered[(j + 1) % UNROLL], (k if j < 3 else k + 1) * (16 * G))
                    stage_scat(g + 1, (j + 1) % UNROLL)
                for t in range(G):
                    pool.indirect_dma_start(out, bass.IndirectOffsetOnAxis(ap=scat_stage[:, j, t:t + 1], axis=0),
                                            rows_out[:, j, t * D:(t + 1) * D], None,
                                            bounds_check=N_NODES - 1, oob_is_err=False)\
                        .then_inc(scattered[j], 16)

            steps(pool, scatter, GROUPS, GROUPS // UNROLL)
            for j in range(UNROLL):
                pool.wait_ge(scattered[j], len(range(j, GROUPS, UNROLL)) * 16 * G)

        @block.scalar
        def _(act):
            def const(dst, src):
                act.dma_start(dst, src).then_inc(consts_loaded, 16)

            def bcast(name, n):
                return a[name].rearrange("(o n) -> o n", o=1).to_broadcast([P, n])

            for t, name in ((bo_b, "bo"), (beta_b, "beta"), (gamma_b, "gamma")):
                const(t[:, :], bcast(name, D))
            for t, name in ((Wq, "Wq"), (Wk, "Wk"), (Wv, "Wv"), (Wo, "Wo")):
                const(t[:, :], a[name])
            const(bq[:, :], a["bq"].rearrange("(p o) -> p o", o=1))
            for t, name in ((bk, "bk"), (bv, "bv"), (bo, "bo"), (beta, "beta")):
                const(t[:, :], a[name].rearrange("(p o) -> p o", o=1))
            for t, name in ((be_b, "be"), (bc2_b, "bc2"), (bd2_b, "bd2")):
                const(t[:, :], bcast(name, HEADS))
            for i in range(G):
                const(bc1[i * CONS_H:(i + 1) * CONS_H, :], a["bc1"].rearrange("(p o) -> p o", o=1))
                const(bd1[i * DIST_H:(i + 1) * DIST_H, :], a["bd1"].rearrange("(p o) -> p o", o=1))
            act.wait_ge(zeroed, 2)
            for i in range(G):
                const(Wc1s[i:i + 1, i * CONS_H:(i + 1) * CONS_H], a["Wc1"])
                const(Wd1s[i:i + 1, i * DIST_H:(i + 1) * DIST_H], a["Wd1"])
                const(Wc2s[i * CONS_H:(i + 1) * CONS_H, i * HEADS:(i + 1) * HEADS], a["Wc2"])
                const(Wd2s[i * DIST_H:(i + 1) * DIST_H, i * HEADS:(i + 1) * HEADS], a["Wd2"])
            for i in range(2):
                const(We2[i * E_DIM:(i + 1) * E_DIM, i * HEADS:(i + 1) * HEADS], a["We"])
            act.wait_ge(consts_loaded, CONST_DMAS * 16)

            def normalise(dst, src, norm, w, rows, done):
                for r in range(rows):
                    last = act.activation(dst[0:w, r * D:(r + 1) * D], src[0:w, r * D:(r + 1) * D], ACT.Identity,
                                          scale=norm[0:w, 0, r:r + 1], bias=norm[0:w, 1, r:r + 1])
                last.then_inc(done, 1)

            def deviation(tmp, w, rows, done):
                act.activation(tmp[0:w, 4, 0:rows], tmp[0:w, 3, 0:rows], ACT.Sqrt, bias=eps[0:w, 0:1]).then_inc(done, 1)

            def step(i, k, j):
                g = half(k, j)
                if j % 2 == 0 and there(g, GROUPS):
                    act.wait_ge(turned, g + 1)
                    act.activation(xdT[:, bass.ds(g * GE, GE)], bank_xd, ACT.Copy)
                    act.activation(xsT[:, :], bank_xs, ACT.Copy)
                    act.activation(eaT[:, :], bank_ea[:, 0:2 * P], ACT.Copy)
                    act.activation(cdT[:, :], bank_ea[0:G, 2 * P:4 * P], ACT.Copy).then_inc(turned_kept, 1)
                if there(i - 1, CHUNKS):
                    act.wait_ge(norm1_ready, i)
                    q = (j - 1) % UNROLL
                    normalise(y[:, q, :], y[:, q, :], norm1[:, q % 2, :, :], width(i - 1), ROWS, u_ready)
                if there(i, CHUNKS):
                    act.wait_ge(var1_ready, i + 1)
                    deviation(tmp1[:, j % 2, :, :], width(i), ROWS, std1_ready)
                if there(i - 4, CHUNKS):
                    act.wait_ge(norm2_ready, i - 3)
                    after(act, out_stored[j % 2], (half(k, j) - 2) * 16)
                    normalise(o[:, j % 2, :], z_ps[j % 2].rearrange("p a b -> p (a b)"),
                              norm2[:, j % 2, :, :], width(i - 4), ROWS, out_ready)
                if j % 2 == 0 and there(g, GROUPS):
                    act.wait_ge(qk_ready, g + 1)
                    act.activation(qT[:, :], bank_xs, ACT.Identity, bias=bq[:, 0:1]).then_inc(q_kept, 1)
                    act.wait_ge(hidden_ps, g + 1)
                    act.activation(h1[:, :], bank_ea[:, 0:P], ACT.Relu, bias=bc1[:, 0:1])
                    act.activation(h2[:, :], bank_ea[0:G * DIST_H, P:2 * P], ACT.Relu, bias=bd1[:, 0:1])\
                        .then_inc(hidden_kept, 1)
                if there(i - 3, CHUNKS):
                    act.wait_ge(var2_ready, i - 2)
                    deviation(tmp2[:, (j - 3) % 2, :, :], width(i - 3), ROWS, std2_ready)

            steps(act, step, CHUNKS + 4, CHUNKS // UNROLL - 1)

            act.wait_ge(scores_ready, GROUPS)
            act.activation(cons_all[:, :, :], cons_all[:, :, :], ACT.Sigmoid).then_inc(sig_ready, 1)
            act.wait_ge(shifted, 1)
            flat = scores[:, :, :].rearrange("p h t -> p (h t)")
            act.activation(flat, flat, ACT.Exp).then_inc(exp_ready, 1)

            act.wait_ge(S_ready, 1)

            def step2(s, k, j):
                if there(s, GROUPS):
                    q = j % 2
                    after(act, v_ready, s - 1)
                    S = scores[:, :, bass.ds(s * G, G)].rearrange("p h t -> p t h")
                    act.activation(sx[:, q, :].rearrange("p (t h d) -> p t h d", t=G, h=HEADS),
                                   S[:, :, :, None].to_broadcast([P, G, HEADS, HEAD_DIM]), ACT.Copy)\
                       .then_inc(sx_ready, 1)
                    after(act, agg_ready, s - 1)
                    act.wait_ge(v_ready, s + 1)
                    act.activation(vT[:, q, :], V_ps, ACT.Identity, bias=bv[:, 0:1]).then_inc(v_kept, 1)
                if there(s - 1, GROUPS):
                    q = (j - 1) % 2
                    act.wait_ge(yT_ps, s)
                    act.activation(yT[:, q, :], YT_ps[q], ACT.Identity, bias=bo[:, 0:1]).then_inc(yT_ready, 1)
                if there(s - 3, GROUPS):
                    q = (j - 3) % 2
                    after(act, z2_ready, s - 4)
                    act.activation(xbT[:, q, :], xdT[:, bass.ds((s - 3) * GE, GE)], ACT.Identity,
                                   bias=beta[:, 0:1]).then_inc(xb_ready, 1)
                    act.wait_ge(norm3_ready, s - 2)
                    normalise(u[:, q, :], Y_ps[q], norm1[:, q, :, :], P, G, u2_ready)
                if there(s - 2, GROUPS):
                    act.wait_ge(var1_ready, s - 1 + CHUNKS)
                    deviation(tmp1[:, j % 2, :, :], P, G, std1_ready)
                if there(s - 6, GROUPS):
                    act.wait_ge(norm4_ready, s - 5)
                    if isinstance(s, int) and s == 6:
                        for slot in range(2):
                            act.wait_ge(out_stored[slot], CHUNKS // 2 * 16)
                    after(act, scattered[(j - 6) % UNROLL], (k - (1 if j >= 2 else 2)) * (16 * G))
                    normalise(rows_out[:, (j - 6) % UNROLL, :], Z_ps[j % 2], norm2[:, j % 2, :, :], P, G, rows_ready)
                if there(s - 5, GROUPS):
                    act.wait_ge(var2_ready, s - 4 + CHUNKS)
                    deviation(tmp2[:, (j - 5) % 2, :, :], P, G, std2_ready)

            steps(act, step2, GROUPS + 6, GROUPS // UNROLL, 3)

        @block.vector
        def _(dve):
            done = [0]

            def link(ins, s=setup_step):
                done[0] += 1
                ins.then_inc(s, 1)
                dve.wait_ge(s, done[0])

            dve.wait_ge(idx_loaded, 80)
            dve.tensor_copy(dst_f[:, :], dst_i[:, :])
            link(dve.tensor_copy(prev_f[:, :], prev_i[:, :]))
            dve.tensor_tensor(unsorted_t[:, :], prev_f[:, :], dst_f[:, :], ALU.is_gt)
            dve.tensor_tensor(same[:, :], prev_f[:, :], dst_f[:, :], ALU.is_equal)
            dve.tensor_scalar(in_first[:, :], dst_f[:, :], dst_f[:, 0:1], None, ALU.is_equal)
            link(dve.tensor_scalar(in_last[:, :], dst_f[:, :], dst_f[:, TILES - 1:TILES], None, ALU.is_equal))
            dve.tensor_reduce(unsorted_p[:, :], unsorted_t[:, :], AX.X, ALU.add)
            dve.tensor_scalar(neg_first[:, :], in_first[:, :], -1.0, BIG, ALU.add, ALU.mult)
            dve.tensor_scalar(neg_last[:, :], in_last[:, :], -1.0, BIG, ALU.add, ALU.mult)
            same_b = same[:, None, :].to_broadcast([P, HEADS, TILES])
            dve.tensor_copy(heads(cont_f)[:, :, 1:TILES], same_b[:, :, 1:TILES])
            dve.memset(heads(cont_f)[:, :, 0:1], 0.0)
            dve.memset(cont[:, HT:HT + 1], 0.0)
            dve.tensor_copy(link8[:, 0, :], same[:, 0:1].to_broadcast([P, HEADS]))
            dve.tensor_copy(link8[:, 1, :], in_first[:, TILES - 1:TILES].to_broadcast([P, HEADS]))
            link(dve.tensor_scalar(rep_f[:, :], same[:, :], -1.0, 1.0, ALU.mult, ALU.add))
            link(dve.scalar_tensor_tensor(scat_f[:, :], dst_f[:, :], -NO_ROW, rep_f[:, :], ALU.add, ALU.mult))
            link(dve.tensor_scalar(scat_f[:, :], scat_f[:, :], NO_ROW, None, ALU.add))
            link(dve.tensor_copy(scat_i[:, :], scat_f[:, :]))
            dve.memset(mul_r[:, :, :], 0.0).then_inc(masks_made_pe, 1)

            dve.wait_ge(consts_loaded, CONST_DMAS * 16)
            dve.wait_ge(ident_made, 7)
            link(dve.tensor_copy(part_bf[:, 0, :], beta_b[:, :]))
            link(dve.tensor_tensor(part_f[:, 0, :], beta_b[:, :], part_bf[:, 0, :], ALU.subtract))
            link(dve.tensor_copy(part_bf[:, 1, :], part_f[:, 0, :]))
            link(dve.tensor_tensor(part_f[:, 1, :], part_f[:, 0, :], part_bf[:, 1, :], ALU.subtract))
            link(dve.tensor_copy(part_bf[:, 2, :], part_f[:, 1, :]))
            link(dve.tensor_scalar(part_f[:, 0, :], part_bf[:, 0, :], ident[:, 0:1], None, ALU.mult))
            link(dve.scalar_tensor_tensor(part_f[:, 1, :], part_bf[:, 1, :], ident[:, 1:2], part_f[:, 0, :],
                                          ALU.mult, ALU.add))
            link(dve.scalar_tensor_tensor(part_f[:, 0, :], part_bf[:, 2, :], ident[:, 2:3], part_f[:, 1, :],
                                          ALU.mult, ALU.add))
            dve.tensor_copy(beta_rows[:, :].rearrange("p (a d) -> p a d", d=D),
                            part_f[:, 0:1, :].to_broadcast([P, G, D])).then_inc(beta_split, 1)

            dve.wait_ge(links_turned, 1)
            dve.tensor_copy(unsorted_i[:, :], bank_sc[:, 256:257]).then_inc(masks_made, 1)
            link(dve.tensor_copy(link_r[:, :, :], bank_sc[0:HEADS, 0:256].rearrange("p (a b) -> p a b", a=2)))
            linked, whole = link_r[:, 0, :], link_r[:, 1, :]
            dve.tensor_tensor(mul_r[:, 0, 1:P], linked[:, 1:P], whole[:, 0:P - 1], ALU.mult)
            dve.tensor_tensor(mul_r[:, 1, 0:P - 1], linked[:, 1:P], whole[:, 1:P], ALU.mult)
            dve.tensor_copy(mul_r[:, 2, 1:P], linked[:, 1:P])
            link(dve.tensor_copy(mul_r[:, 3, 0:P - 1], linked[:, 1:P]))
            link(dve.tensor_scalar(neg_r[:, :, :], mul_r[:, :, :], -1.0, BIG, ALU.add, ALU.mult))

            def statistics(src, st, tmp, w, rows, step_sem, c, var_sem):
                for r in range(rows):
                    last = dve.bn_stats(st[0:w, r, :], src[0:w, r * D:(r + 1) * D])
                last.then_inc(step_sem, 1)
                dve.wait_ge(step_sem, c + 1)
                mean_e, mean_o = st[0:w, 0:rows, 1], st[0:w, 0:rows, 4]
                sq_e, sq_o = st[0:w, 0:rows, 2], st[0:w, 0:rows, 5]
                two_mean, diff, sq, var = (tmp[0:w, n, 0:rows] for n in range(4))
                dve.tensor_tensor(diff, mean_e, mean_o, ALU.subtract)
                dve.tensor_tensor(sq, sq_e, sq_o, ALU.add)
                dve.tensor_tensor(two_mean, mean_e, mean_o, ALU.add).then_inc(step_sem, 1)
                dve.wait_ge(step_sem, c + 2)
                dve.scalar_tensor_tensor(diff, diff, 0.25, diff, ALU.mult, ALU.mult).then_inc(step_sem, 1)
                dve.wait_ge(step_sem, c + 3)
                dve.scalar_tensor_tensor(var, sq, 1.0 / D, diff, ALU.mult, ALU.add).then_inc(var_sem, 1)

            def factors(tmp, norm, w, rows, inv_sem, c, done_sem):
                dve.reciprocal(norm[0:w, 0, 0:rows], tmp[0:w, 4, 0:rows]).then_inc(inv_sem, 1)
                dve.wait_ge(inv_sem, c + 1)
                dve.scalar_tensor_tensor(norm[0:w, 1, 0:rows], tmp[0:w, 0, 0:rows], -0.5, norm[0:w, 0, 0:rows],
                                         ALU.mult, ALU.mult).then_inc(done_sem, 1)

            def times_gamma(buf, w, rows, done_sem):
                v = buf[0:w, :].rearrange("p (r d) -> p r d", d=D)
                dve.tensor_tensor(v, v, gamma_b[0:w, None, :].to_broadcast([w, rows, D]), ALU.mult)\
                   .then_inc(done_sem, 1)

            def step(i, k, j):
                g = half(k, j)
                if there(i - 4, CHUNKS):
                    dve.wait_ge(std2_ready, i - 3)
                    factors(tmp2[:, j % 2, :, :], norm2[:, j % 2, :, :], width(i - 4), ROWS,
                            inv2_ready, i - 4, norm2_ready)
                if there(i, CHUNKS):
                    dve.wait_ge(y_ready, i + 1)
                    statistics(y[:, j, :], st1[:, j % 2, :, :], tmp1[:, j % 2, :, :], width(i), ROWS,
                               stat1, i * 3, var1_ready)
                if there(i - 2, CHUNKS):
                    dve.wait_ge(u_ready, i - 1)
                    times_gamma(y[:, (j - 2) % UNROLL, :], width(i - 2), ROWS, ug_ready)
                if there(i - 3, CHUNKS):
                    dve.wait_ge(z_ready, i - 2)
                    q = (j - 3) % 2
                    statistics(z_ps[q].rearrange("p a b -> p (a b)"), st2[:, q, :, :], tmp2[:, q, :, :],
                               width(i - 3), ROWS, stat2, (i - 3) * 3, var2_ready)
                if there(i, CHUNKS):
                    dve.wait_ge(std1_ready, i + 1)
                    factors(tmp1[:, j % 2, :, :], norm1[:, j % 2, :, :], width(i), ROWS,
                            inv1_ready, i, norm1_ready)
                if j % 2 == 0 and there(g, GROUPS):
                    dve.wait_ge(q_kept, g + 1)
                    dve.scalar_tensor_tensor(prod[:, :], bank_xd, bk[:, 0:1], qT[:, :], ALU.add, ALU.mult)\
                       .then_inc(prod_ready, 1)
                if j % 2 == 1 and there(g, GROUPS):
                    dve.wait_ge(parts_ps, g + 1)
                    for n, (dst, bias) in enumerate(((scores, be_b), (cons_all, bc2_b), (dist_all, bd2_b))):
                        last = dve.tensor_tensor(
                            dst[:, :, bass.ds(g * G, G)],
                            bank_sc[:, n * G * HEADS:(n + 1) * G * HEADS].rearrange("p (t h) -> p h t", h=HEADS),
                            bias[:, :, None].to_broadcast([P, HEADS, G]), ALU.add)
                    last.then_inc(scores_ready, 1)

            steps(dve, step, CHUNKS + 4, CHUNKS // UNROLL - 1)

            dve.wait_ge(sig_ready, 1)
            done[0] = 0
            link(dve.tensor_tensor(scores[:, :, :], scores[:, :, :], cons_all[:, :, :], ALU.mult), soft_step)
            link(dve.tensor_tensor(scores[:, :, :], scores[:, :, :], dist_all[:, :, :], ALU.add), soft_step)

            flat = scores[:, :, :].rearrange("p h t -> p (h t)")

            def soft(ins):
                link(ins, soft_step)

            def segments(n, first_mask, op0, op, start, masks_r, comb0, in_masks):
                soft(dve.tensor_tensor_scan(run, first_mask, flat, start, op0, op))
                soft(dve.scalar_tensor_tensor(ends, cont_b, 0.0, run, ALU.is_equal, ALU.mult))
                soft(dve.tensor_tensor_scan(total[:, ::-1], cont_b[:, ::-1], ends[:, ::-1], 0.0,
                                            ALU.mult, ALU.add))
                dve.sem_inc(edges_out, 1)
                dve.wait_ge(edges_turned, n + 1)
                first_r, last_r = bank_sc[0:HEADS, 0:P], bank_sc[0:HEADS, P:2 * P]
                dve.tensor_tensor(edge_r[:, 0, 1:P], last_r[:, 0:P - 1], masks_r[:, 2, 1:P], comb0)
                dve.tensor_tensor(edge_r[:, 1, 0:P - 1], first_r[:, 1:P], masks_r[:, 3, 0:P - 1], comb0)
                dve.memset(edge_r[:, 0, 0:1], start)
                soft(dve.memset(edge_r[:, 1, P - 1:P], start))
                dve.tensor_tensor_scan(carry_r[:, 0, :], masks_r[:, 0, :], edge_r[:, 0, :], start, op0, op)
                dve.tensor_tensor_scan(carry_r[:, 1, ::-1], masks_r[:, 1, ::-1], edge_r[:, 1, ::-1], start, op0, op)\
                   .then_inc(carries_out, 1)
                dve.wait_ge(carries_turned, n + 1)
                soft(dve.tensor_copy(carry[:, :, :], bank_sc[:, 256:256 + 2 * HEADS]
                                     .rearrange("p (a b) -> p a b", a=2)))
                th = heads(total)
                for side in range(2):
                    for h in range(HEADS):
                        last = dve.scalar_tensor_tensor(th[:, h, :], in_masks[side][:, :], carry[:, side, h:h + 1],
                                                        th[:, h, :], comb0, op)
                    soft(last)
                dve.sem_inc(fast_done, 1)
                dve.wait_ge(reduced, n + 1)

            soft(dve.tensor_scalar(neg_f, cont_f, -1.0, BIG, ALU.add, ALU.mult))
            segments(0, neg_f, ALU.add, ALU.max, -BIG, neg_r, ALU.add, (neg_first, neg_last))
            dve.tensor_tensor(flat, flat, total, ALU.subtract).then_inc(shifted, 1)
            dve.wait_ge(exp_ready, 1)
            segments(1, cont_f, ALU.mult, ALU.add, 0.0, mul_r, ALU.mult, (in_first, in_last))
            soft(dve.reciprocal(run, total))
            dve.tensor_tensor(flat, total, run, ALU.mult).then_inc(S_ready, 1)
            dve.wait_ge(S_ready, 1)

            def step2(s, k, j):
                q = j % 2
                if there(s - 6, GROUPS):
                    dve.wait_ge(std2_ready, s - 5 + CHUNKS)
                    factors(tmp2[:, q, :, :], norm2[:, q, :, :], P, G, inv2_ready, s - 6 + CHUNKS, norm4_ready)
                if there(s, GROUPS):
                    dve.wait_ge(v_kept, s + 1)
                    dve.tensor_tensor(aggT[:, q, :], vT[:, q, :], S_ps, ALU.mult).then_inc(agg_ready, 1)
                if there(s - 2, GROUPS):
                    dve.wait_ge(y2_ready, s - 1)
                    statistics(Y_ps[q], st1[:, q, :, :], tmp1[:, q, :, :], P, G,
                               stat1, (s - 2) * 3 + 3 * CHUNKS, var1_ready)
                if there(s - 4, GROUPS):
                    dve.wait_ge(u2_ready, s - 3)
                    times_gamma(u[:, q, :], P, G, ug2_ready)
                if there(s - 5, GROUPS):
                    dve.wait_ge(z2_ready, s - 4)
                    statistics(Z_ps[1 - q], st2[:, 1 - q, :, :], tmp2[:, 1 - q, :, :], P, G,
                               stat2, (s - 5) * 3 + 3 * CHUNKS, var2_ready)
                if there(s - 2, GROUPS):
                    dve.wait_ge(std1_ready, s - 1 + CHUNKS)
                    factors(tmp1[:, q, :, :], norm1[:, q, :, :], P, G, inv1_ready, s - 2 + CHUNKS, norm3_ready)

            steps(dve, step2, GROUPS + 6, GROUPS // UNROLL, 3)

        @block.tensor
        def _(pe):
            pe.wait_ge(ident_made, 7)
            pe.wait_ge(masks_made_pe, 1)
            pe.transpose(bank_sc[0:HEADS, 0:P], link8[:, 0, :], ident[:, :])
            pe.transpose(bank_sc[0:HEADS, P:2 * P], link8[:, 1, :], ident[:, :])
            pe.matmul(bank_sc[:, 256:257], ones[:, :], unsorted_p[:, :], start=True, stop=True)\
              .then_inc(links_turned, 1)
            pe.wait_ge(consts_loaded, CONST_DMAS * 16)
            pe.wait_ge(beta_split, 1)
            pe.wait_ge(masks_made, 1)

            def dense_z(i, j):
                w = width(i)
                s = j % 2
                pe.wait_ge(ug_ready, i + 1)
                after(pe, out_ready, i - 1)
                for c in range(2):
                    cols = slice(c * 512, (c + 1) * 512)
                    pe.matmul(z_ps[s][0:w, c, :], ones_bf[:, 0:w], beta_rows[:, :],
                              start=True, stop=False)
                    pe.matmul(z_ps[s][0:w, c, :], ident[0:w, 0:w], x_in[0:w, j, cols], start=False, stop=False)
                    last = pe.matmul(z_ps[s][0:w, c, :], ident[0:w, 0:w], y[0:w, j, cols], start=False, stop=True)
                last.then_inc(z_ready, 1)

            def step(i, k, j):
                g = half(k, j)
                s = j // 2
                if j % 2 == 0 and there(g, GROUPS):
                    pe.wait_ge(gathered[s], (k + 1) * (16 * 2 * G))
                    pe.wait_ge(ea_loaded[s], (k + 1) * 16)
                    pe.wait_ge(dist_staged, g + 1)
                    after(pe, q_kept, g)
                    after(pe, prod_ready, g)
                    after(pe, hidden_kept, g)
                    for t in range(G):
                        pe.transpose(bank_xd[:, t * P:(t + 1) * P], xd[:, s, t, 0:D], ident[:, :])
                    for t in range(G):
                        pe.transpose(bank_xs[:, t * P:(t + 1) * P], xs[:, s, t, :], ident[:, :])
                    for t in range(2):
                        pe.transpose(bank_ea[:, t * P:(t + 1) * P], ea[:, s, t * P:(t + 1) * P], ident[:, :])
                    pe.transpose(bank_ea[0:G, 2 * P:3 * P], xd[:, s, :, D], ident[:, :])
                    pe.transpose(bank_ea[0:G, 3 * P:4 * P], dist_s[:, s, :], ident[:, :])\
                      .then_inc(turned, 1)
                if j % 2 == 0 and there(g, GROUPS):
                    pe.wait_ge(turned_kept, g + 1)
                    pe.matmul(bank_xs, Wq[:, :], xsT[:, :], start=True, stop=True)
                    pe.matmul(bank_xd, Wk[:, :], xdT[:, bass.ds(g * GE, GE)], start=True, stop=True)\
                      .then_inc(qk_ready, 1)
                    pe.matmul(bank_ea[:, 0:P], Wc1s[:, :], cdT[:, 0:P], start=True, stop=True)
                    pe.matmul(bank_ea[0:G * DIST_H, P:2 * P], Wd1s[:, :], cdT[:, P:2 * P], start=True, stop=True)\
                      .then_inc(hidden_ps, 1)
                if j % 2 == 1 and there(g, GROUPS):
                    pe.wait_ge(prod_ready, g + 1)
                    pe.wait_ge(hidden_kept, g + 1)
                    after(pe, scores_ready, g)
                    for t in range(2):
                        pe.matmul(bank_sc[:, t * 2 * HEADS:(t + 1) * 2 * HEADS], eaT[:, t * P:(t + 1) * P], We2[:, :],
                                  start=True, stop=False)
                        for c in range(2):
                            pe.matmul(bank_sc[:, t * 2 * HEADS:(t + 1) * 2 * HEADS],
                                      prod[:, (2 * t + c) * P:(2 * t + c + 1) * P],
                                      head_sel3[:, (1 - c) * HEADS:(3 - c) * HEADS], start=False, stop=c == 1)
                    pe.matmul(bank_sc[:, G * HEADS:2 * G * HEADS], h1[:, :], Wc2s[:, :], start=True, stop=True)
                    pe.matmul(bank_sc[:, 2 * G * HEADS:3 * G * HEADS], h2[:, :], Wd2s[:, :], start=True, stop=True)\
                      .then_inc(parts_ps, 1)
                if there(i - 2, CHUNKS):
                    dense_z(i - 2, (j - 2) % UNROLL)

            steps(pe, step, CHUNKS + 2, CHUNKS // UNROLL - 1)

            th = heads(total)
            for n in range(2):
                pe.wait_ge(edges_out, n + 1)
                pe.transpose(bank_sc[0:HEADS, 0:P], th[:, :, 0], ident[:, :])
                pe.transpose(bank_sc[0:HEADS, P:2 * P], th[:, :, TILES - 1], ident[:, :]).then_inc(edges_turned, 1)
                pe.wait_ge(carries_out, n + 1)
                for side in range(2):
                    last = pe.transpose(bank_sc[:, 256 + side * HEADS:256 + (side + 1) * HEADS], carry_r[:, side, :],
                                        ident[0:HEADS, 0:HEADS])
                last.then_inc(carries_turned, 1)

            def step2(s, k, j):
                q = j % 2
                if there(s, GROUPS):
                    pe.wait_ge(sx_ready, s + 1)
                    after(pe, agg_ready, s)
                    for t in range(G):
                        pe.transpose(S_ps[:, t * P:(t + 1) * P], sx[:, q, t * P:(t + 1) * P], ident[:, :])
                    pe.matmul(V_ps, Wv[:, :], xdT[:, bass.ds(s * GE, GE)], start=True, stop=True)\
                      .then_inc(v_ready, 1)
                if there(s - 1, GROUPS):
                    pe.wait_ge(agg_ready, s)
                    after(pe, yT_ready, s - 2)
                    pe.matmul(YT_ps[1 - q], ident[:, :], xdT[:, bass.ds((s - 1) * GE, GE)], start=True, stop=False)
                    pe.matmul(YT_ps[1 - q], Wo[:, :], aggT[:, 1 - q, :], start=False, stop=True).then_inc(yT_ps, 1)
                if there(s - 2, GROUPS):
                    pe.wait_ge(yT_ready, s - 1)
                    after(pe, u2_ready, s - 3)
                    for t in range(G):
                        last = pe.transpose(Y_ps[q][:, t * P:(t + 1) * P], yT[:, q, t * P:(t + 1) * P], ident[:, :])
                    last.then_inc(y2_ready, 1)
                if there(s - 4, GROUPS):
                    pe.wait_ge(ug2_ready, s - 3)
                    pe.wait_ge(xb_ready, s - 3)
                    after(pe, rows_ready, s - 5)
                    for t in range(G):
                        pe.matmul(Z_ps[q][:, t * P:(t + 1) * P], xbT[:, q, t * P:(t + 1) * P], ident[:, :],
                                  start=t == 0, stop=False, skip_group_check=True)
                    pe.matmul(Z_ps[q], ident[:, :], u[:, q, :], start=False, stop=True,
                              skip_group_check=True).then_inc(z2_ready, 1)

            steps(pe, step2, GROUPS + 6, GROUPS // UNROLL, 3)


_WEIGHTS = ["Wq", "bq", "Wk", "bk", "Wv", "bv", "We", "be", "Wc1", "bc1", "Wc2", "bc2", "Wd1", "bd1", "Wd2", "bd2",
            "Wo", "bo", "gamma", "beta"]
CONST_DMAS = 2 + 1 + 4 + 5 + 3 + 2 * G + 4 * G + 2


def kernel(**inputs):
    import numpy as _np
    import concourse.bacc as _bacc
    from concourse import mybir as _mybir
    from concourse.bass_utils import run_bass_kernel_spmd as _run

    nc = _bacc.Bacc("TRN2", target_bir_lowering=False, num_devices=1)
    pad = PAD_EDGES - N_EDGES

    def padded(v, fill):
        tail = _np.full((pad,) + v.shape[1:], fill, v.dtype)
        return _np.concatenate([v, tail])

    x = _np.asarray(inputs["x"])
    xn = _np.concatenate([x, _np.asarray(inputs["node_vec1"])], axis=1)
    xn = _np.concatenate([xn, _np.zeros((1, XN), x.dtype)])
    data = {
        "x": x, "xn": xn,
        "src": padded(_np.asarray(inputs["src"]), 0),
        "dst": padded(_np.asarray(inputs["dst"]), N_NODES),
        "edge_attr": padded(_np.asarray(inputs["edge_attr_64"]), 0),
        "edge_weight": padded(_np.asarray(inputs["edge_weight1"]).reshape(-1), 0),
    }
    for name in _WEIGHTS:
        data[name] = _np.asarray(inputs["L0_gnn_" + name])
    arrays, args = {}, {}
    for name, v in data.items():
        v = _np.ascontiguousarray(v)
        arrays[f"in_{name}_dram"] = v
        args[name] = nc.dram_tensor(f"in_{name}_dram", v.shape, _mybir.dt.from_np(v.dtype), kind="ExternalInput").ap()
    out = nc.dram_tensor("out_0_dram", (N_NODES, D), _mybir.dt.float32, kind="ExternalOutput").ap()
    gnn_kernel(nc, args, out)
    r = _run(nc, [arrays], core_ids=[0])
    return r.results[0]["out_0_dram"]
```

```python
from contextlib import ExitStack

import concourse.bass as bass
from concourse import mybir

F32 = mybir.dt.float32
BF16 = mybir.dt.bfloat16
I32 = mybir.dt.int32
ALU = mybir.AluOpType
ACT = mybir.ActivationFunctionType
AX = mybir.AxisListType

P = 128
N_NODES = 100000
D = 128
E_DIM = 64
HEADS = 8
HEAD_DIM = D // HEADS
CONS_H = 32
DIST_H = 16
N_EDGES = 25000
TILES = -(-N_EDGES // P)
PAD_EDGES = P * TILES
G = 4
GROUPS = TILES // G
GE = G * P
XN = D + 1
ROWS = 8
DVE_ROWS = 3
CW = ROWS * D
CHUNK = P * ROWS
FULL_CHUNKS = N_NODES // CHUNK
REST_P = (N_NODES - FULL_CHUNKS * CHUNK) // ROWS
CHUNKS = FULL_CHUNKS + 1
UNROLL = 4
SLOTS2 = 8
PEELED = 2
JOINT2 = CHUNKS + 2 - 3
EPS = 1e-5
BIG = 3e38
NO_ROW = 131072.0
assert TILES % G == 0 and REST_P * ROWS + FULL_CHUNKS * CHUNK == N_NODES
assert CHUNKS == 2 * GROUPS and GROUPS == 12 * UNROLL + 1 and E_DIM * 2 == P


def after(engine, sem, count):
    if not isinstance(count, int) or count > 0:
        engine.wait_ge(sem, count)


class Memory:
    pass


def gnn_kernel(nc, a, out):
    ctx = ExitStack()
    with ctx:
        m = Memory()

        def sb(name, shape, dt=F32):
            return ctx.enter_context(nc.sbuf_tensor(name, shape, dt))

        def sem(name):
            return ctx.enter_context(nc.semaphore(name))

        ident = sb("ident", [P, P])
        eps = sb("eps", [P, 1])
        ones = sb("ones", [P, P])
        ones_bf = sb("ones_bf", [P, P], BF16)
        Wq = sb("Wq", [P, D])
        Wk = sb("Wk", [P, D])
        Wv = sb("Wv", [P, D])
        Wo = sb("Wo", [P, D])
        bq = sb("bq", [P, 1])
        bk = sb("bk", [P, 1])
        head_sel3 = sb("head_sel3", [P, 3 * HEADS])
        head_sel = head_sel3[:, HEADS:2 * HEADS]
        We2 = sb("We2", [P, 2 * HEADS])
        Wc1s = sb("Wc1s", [G, G * CONS_H])
        Wd1s = sb("Wd1s", [G, G * DIST_H])
        Wc2s = sb("Wc2s", [G * CONS_H, G * HEADS])
        Wd2s = sb("Wd2s", [G * DIST_H, G * HEADS])
        bc1 = sb("bc1", [G * CONS_H, 1])
        bd1 = sb("bd1", [G * DIST_H, 1])
        be_b = sb("be_b", [P, HEADS])
        bc2_b = sb("bc2_b", [P, HEADS])
        bd2_b = sb("bd2_b", [P, HEADS])
        gamma_b = sb("gamma_b", [P, D])
        bo_b = sb("bo_b", [P, D])
        bias_rows = sb("bias_rows", [P, 3, D], BF16)
        beta_rows, bo_rows, bv_rows = (bias_rows[:, n:n + 1, :].to_broadcast([P, G, D]) for n in range(3))
        src_i = sb("src_i", [P, TILES], I32)
        dst_i = sb("dst_i", [P, TILES], I32)
        dist = sb("dist", [P, TILES])
        dst_f = sb("dst_f", [P, TILES])
        unsorted_p = sb("unsorted_p", [P, 1])
        unsorted_i = sb("unsorted_i", [P, 1], I32)
        same = sb("same", [P, TILES])
        cont = sb("cont", [P, HEADS * TILES + 1])
        in_first = sb("in_first", [P, TILES])
        in_last = sb("in_last", [P, TILES])
        neg_first = sb("neg_first", [P, TILES])
        neg_last = sb("neg_last", [P, TILES])
        link8 = sb("link8", [P, 2, HEADS])
        link_r = sb("link_r", [HEADS, 2, P])
        mul_r = sb("mul_r", [HEADS, 4, P])
        neg_r = sb("neg_r", [HEADS, 4, P])
        edge_r = sb("edge_r", [HEADS, 2, P])
        carry_r = sb("carry_r", [HEADS, 2, P])
        carry = sb("carry", [P, 2, HEADS])
        rep_f = sb("rep_f", [P, TILES])
        scat_f = sb("scat_f", [P, TILES])
        scat_i = sb("scat_i", [P, TILES], I32)
        x_in = sb("x_in", [P, UNROLL, CW])
        y = sb("y", [P, UNROLL, CW])
        o = sb("o", [P, 2, CW])
        st = sb("st", [P, 2, 2, ROWS, 6])
        tmp = sb("tmp", [P, 2, 5, 2, ROWS])
        norm = sb("norm", [P, 2, 2, 2, ROWS])
        xs = sb("xs", [P, 2, G, D])
        xd = sb("xd", [P, 2, G, XN])
        st1, st2 = st[:, :, 0], st[:, :, 1]
        tmp1, tmp2 = tmp[:, :, :, 0], tmp[:, :, :, 1]
        norm1, norm2 = norm[:, :, :, 0], norm[:, :, :, 1]
        idx = sb("idx", [P, 2, 2, G], I32)
        dist_s = sb("dist_s", [P, 2, G])
        ea = sb("ea", [P, 2, G * E_DIM])
        xsT = sb("xsT", [P, GE])
        xdT = sb("xdT", [P, TILES * P])
        eaT = sb("eaT", [P, 2 * P])
        cdT = sb("cdT", [G, 2 * P])
        qT = sb("qT", [P, GE])
        prod = sb("prod", [P, GE])
        h1 = sb("h1", [G * CONS_H, P])
        h2 = sb("h2", [G * DIST_H, P])
        cons_all = sb("cons_all", [P, HEADS, TILES])
        dist_all = sb("dist_all", [P, HEADS, TILES])
        scores = sb("scores", [P, HEADS, TILES])
        scat_stage = sb("scat_stage", [P, UNROLL, G], I32)

        x_flat = x_in[:, :, :].rearrange("p a b -> p (a b)")
        y_flat = y[:, :, :].rearrange("p a b -> p (a b)")
        o_flat = o[:, :, :].rearrange("p a b -> p (a b)")
        HT = HEADS * TILES
        cont_f = cont[:, 0:HT]
        cont_b = cont[:, 1:HT + 1]
        early = xdT[:, TILES * P - 2560:TILES * P]
        bias_b = early[:, 0:3 * D].rearrange("p (n d) -> p n d", n=3)
        part_f = early[:, 3 * D:9 * D].rearrange("p (s n d) -> p s n d", s=2, n=3)
        part_bf = early[:, 9 * D:15 * D].bitcast(BF16)[:, 0:9 * D] \
            .rearrange("p (s n d) -> p s n d", s=3, n=3)
        prev_f = early[:, 15 * D:15 * D + TILES]
        unsorted_t = early[:, 15 * D + 2 * TILES:15 * D + 3 * TILES]
        prev_i = early[:, 15 * D + TILES:15 * D + 2 * TILES].bitcast(I32)

        def heads(ap):
            return ap.rearrange("p (h t) -> p h t", h=HEADS)

        run = x_flat[:, 0:HT]
        ends = x_flat[:, HT:2 * HT]
        total = y_flat[:, 0:HT]
        neg_f = y_flat[:, HT:2 * HT]
        all_row = y_flat[:, HT:2 * HT]
        all_prod = o_flat[:, 0:HT]
        all_dst = x_flat[:, 2 * HT:2 * HT + TILES]
        all_mask = x_flat[:, 2 * HT + TILES:2 * HT + 2 * TILES]
        all_idx = x_flat[:, 2 * HT + 2 * TILES:2 * HT + 3 * TILES]
        all_less = x_flat[:, 2 * HT + 3 * TILES:2 * HT + 4 * TILES]
        edge_no = o_flat[:, HT:HT + TILES]
        all_count = y_flat[:, 2 * HT:2 * HT + TILES]
        all_col = y_flat[:, 2 * HT + TILES:2 * HT + TILES + 2 + HEADS]
        xg = x_flat.rearrange("p (s n) -> p s n", s=SLOTS2)
        agg, aggT, u = (y_flat[:, 2 * n * GE:2 * (n + 1) * GE].rearrange("p (s n) -> p s n", s=2)
                        for n in range(3))
        rows_out = o_flat.rearrange("p (s n) -> p s n", s=UNROLL)

        scr_rows = nc.dram_tensor("scr_rows", [P, HEADS + 2, TILES], F32).ap()

        banks = [ctx.enter_context(nc.psum_tensor(f"bank{i}", [P, 2, 512], F32)) for i in range(4)]
        z_ps = [banks[0][:, :, :], banks[1][:, :, :]]
        bank_xs = banks[2][:, 0, :]
        bank_xd = banks[2][:, 1, :]
        bank_ea = banks[3][:, 0, :]
        bank_sc = banks[3][:, 1, :]
        V_ps, T_ps, Y_ps, Z_ps = ([bank[:, s, :] for s in range(2)] for bank in banks)

        zeroed = sem("zeroed")
        ident_made = sem("ident_made")
        idx_loaded = sem("idx_loaded")
        consts_loaded = sem("consts_loaded")
        masks_made = sem("masks_made")
        links_turned = sem("links_turned")
        bias_split = sem("bias_split")
        masks_made_pe = sem("masks_made_pe")
        setup_step = sem("setup_step")
        x_loaded = [sem(f"x_loaded{j}") for j in range(UNROLL)]
        y_ready = sem("y_ready")
        stat = sem("stat")
        var_ready = sem("var_ready")
        std_ready = sem("std_ready")
        inv_ready = sem("inv_ready")
        norm_ready = sem("norm_ready")
        rows_normed = sem("rows_normed")
        u_ready = sem("u_ready")
        ug_ready = sem("ug_ready")
        z_ready = sem("z_ready")
        out_ready = sem("out_ready")
        out_stored = [sem(f"out_stored{j}") for j in range(2)]
        idx_staged = sem("idx_staged")
        dist_staged = sem("dist_staged")
        gathered = [sem(f"gathered{j}") for j in range(2)]
        ea_loaded = [sem(f"ea_loaded{j}") for j in range(2)]
        turned = sem("turned")
        turned_kept = sem("turned_kept")
        qk_ready = sem("qk_ready")
        hidden_ps = sem("hidden_ps")
        q_kept = sem("q_kept")
        hidden_kept = sem("hidden_kept")
        prod_ready = sem("prod_ready")
        parts_ps = sem("parts_ps")
        sig_ready = sem("sig_ready")
        scores_ready = sem("scores_ready")
        soft_step = sem("soft_step")
        edges_out = sem("edges_out")
        edges_turned = sem("edges_turned")
        carries_out = sem("carries_out")
        carries_turned = sem("carries_turned")
        fast_done = sem("fast_done")
        reduced = sem("reduced")
        shifted = sem("shifted")
        exp_ready = sem("exp_ready")
        all_dma = sem("all_dma")
        all_step = sem("all_step")
        all_fence = sem("all_fence")
        
        S_ready = sem("S_ready")
        xg_ready = sem("xg_ready")
        v_ready = sem("v_ready")
        agg_turned = sem("agg_turned")
        aggT_ready = sem("aggT_ready")
        agg_ready = sem("agg_ready")
        y2_ready = sem("y2_ready")
        u2_ready = sem("u2_ready")
        ug2_ready = sem("ug2_ready")
        z2_ready = sem("z2_ready")
        rows_ready = sem("rows_ready")
        scat_staged = sem("scat_staged")
        scattered = [sem(f"scattered{j}") for j in range(UNROLL)]

        def width(i):
            return REST_P if isinstance(i, int) and i == CHUNKS - 1 else P

        def chunk_rows(t, i):
            w = width(i)
            return t[bass.ds(i * CHUNK, w * ROWS), :].rearrange("(p r) d -> p (r d)", r=ROWS)

        def x_free(i):
            return i - UNROLL + 1

        def steps(engine, step, last, whole, peeled=PEELED, unroll=UNROLL):
            for i in range(peeled * unroll):
                step(i, i // unroll, i % unroll)
            with engine.Fori(peeled, whole) as k:
                for j in range(unroll):
                    step(k * unroll + j, k, j)
            for i in range(whole * unroll, last):
                step(i, i // unroll, i % unroll)

        def there(i, n):
            return not isinstance(i, int) or 0 <= i < n

        def joint(i, n, lag):
            first, second = there(i, n), there(i - lag, n)
            return slice(0 if first else 1, 2 if second else 1) if first or second else None

        def half(k, j):
            return k * (UNROLL // 2) + j // 2

        ea_v = a["edge_attr"].rearrange("(p t) f -> p (t f)", t=TILES)

        block = ctx.enter_context(nc.Block())

        @block.sync
        def _(sp):
            flat = a["dst"]
            sp.dma_start(src_i[:, :], a["src"].rearrange("(p t) -> p t", t=TILES)).then_inc(idx_loaded, 16)
            sp.dma_start(dst_i[:, :], flat.rearrange("(p t) -> p t", t=TILES)).then_inc(idx_loaded, 16)
            sp.wait_ge(zeroed, 1)
            sp.dma_start(prev_i[1:P, :], flat[TILES - 1:P * TILES - 1].rearrange("(p t) -> p t", t=TILES))\
              .then_inc(idx_loaded, 16)
            sp.dma_start(prev_i[0:1, 1:TILES], flat[0:TILES - 1].rearrange("(p t) -> p t", p=1))\
              .then_inc(idx_loaded, 16)
            sp.dma_start(dist[:, :], a["edge_weight"].rearrange("(p t) -> p t", t=TILES)).then_inc(idx_loaded, 16)

            def load_x(i, k, j):
                after(sp, z_ready, x_free(i))
                w = width(i)
                sp.dma_start(x_in[0:w, j, :], chunk_rows(a["x"], i)).then_inc(x_loaded[j], 16)

            def load_ea(g, s):
                after(sp, turned, g - 1)
                sp.dma_start(ea[:, s, :], ea_v[:, bass.ds(g * (G * E_DIM), G * E_DIM)]).then_inc(ea_loaded[s], 16)

            load_x(0, 0, 0)
            load_ea(0, 0)
            load_x(1, 0, 1)

            def step(i, k, j):
                g = half(k, j)
                if there(i + 2, CHUNKS):
                    load_x(i + 2, k if j < 2 else k + 1, (j + 2) % UNROLL)
                if j % 2 == 0 and there(g + 1, GROUPS):
                    load_ea(g + 1, (j // 2 + 1) % 2)
                if there(i - 3, CHUNKS):
                    sp.wait_ge(out_ready, 2 * i - 4)
                    w = width(i - 3)
                    q = (j - 3) % 2
                    sp.dma_start(chunk_rows(out, i - 3), o[0:w, q, :]).then_inc(out_stored[q], 16)

            steps(sp, step, CHUNKS + 3, CHUNKS // UNROLL - 1)

        @block.gpsimd
        def _(pool):
            pool.memset(prev_i[0:1, 0:1], -1).then_inc(zeroed, 1)
            for t in (We2, Wc1s, Wd1s, Wc2s, Wd2s):
                last = pool.memset(t[:, :], 0.0)
            last.then_inc(zeroed, 1)
            pool.memset(ident[:, :], 0.0).then_inc(ident_made, 1)
            pool.memset(head_sel3[:, :], 0.0).then_inc(ident_made, 1)
            pool.wait_ge(ident_made, 2)
            pool.memset(head_sel, float(HEAD_DIM) ** -0.5).then_inc(ident_made, 1)
            pool.wait_ge(ident_made, 3)
            pool.affine_select(out=ident[:, :], in_=ident[:, :], compare_op=ALU.not_equal, fill=1.0,
                               base=0, pattern=[[-1, P]], channel_multiplier=1).then_inc(ident_made, 1)
            pool.affine_select(out=head_sel, in_=head_sel, compare_op=ALU.is_ge, fill=0.0,
                               base=0, pattern=[[-HEAD_DIM, HEADS]], channel_multiplier=1).then_inc(ident_made, 1)
            pool.wait_ge(ident_made, 5)
            pool.affine_select(out=head_sel, in_=head_sel, compare_op=ALU.is_ge, fill=0.0,
                               base=HEAD_DIM - 1, pattern=[[HEAD_DIM, HEADS]], channel_multiplier=-1)\
                .then_inc(ident_made, 1)
            pool.memset(ones[:, :], 1.0)
            pool.memset(eps[:, :], EPS)
            pool.memset(ones_bf[:, :], 1.0).then_inc(ident_made, 1)

            def stage(g, s):
                pool.tensor_copy(idx[:, s, 0, :], src_i[:, bass.ds(g * G, G)])
                pool.tensor_copy(idx[:, s, 1, :], dst_i[:, bass.ds(g * G, G)]).then_inc(idx_staged, 1)

            def gather_src(s):
                for t in range(G):
                    pool.indirect_dma_start(xs[:, s, t, :], None, a["x"],
                                            bass.IndirectOffsetOnAxis(ap=idx[:, s, 0, t:t + 1], axis=0))\
                        .then_inc(gathered[s], 16)

            def gather_dst(s):
                for t in range(G):
                    pool.indirect_dma_start(xd[:, s, t, :], None, a["xn"],
                                            bass.IndirectOffsetOnAxis(ap=idx[:, s, 1, t:t + 1], axis=0))\
                        .then_inc(gathered[s], 16)

            def add_bo(i, k, j):
                pool.wait_ge(x_loaded[j], k * 16 + 16)
                w = width(i)
                pool.tensor_tensor(
                    y[0:w, j, :].rearrange("p (r d) -> p r d", d=D),
                    x_in[0:w, j, :].rearrange("p (r d) -> p r d", d=D),
                    bo_b[0:w, None, :].to_broadcast([w, ROWS, D]), ALU.add).then_inc(y_ready, 1)

            pool.wait_ge(idx_loaded, 80)
            stage(0, 0)
            stage(1, 1)
            pool.tensor_copy(dist_s[:, 0, :], dist[:, 0:G]).then_inc(dist_staged, 1)
            pool.wait_ge(idx_staged, 2)
            gather_src(0)
            gather_dst(0)
            pool.wait_ge(consts_loaded, CONST_DMAS * 16)

            def step(i, k, j):
                g = half(k, j)
                s = (j // 2 + 1) % 2
                if j % 2 == 0:
                    if there(g + 1, GROUPS):
                        pool.wait_ge(idx_staged, g + 2)
                        after(pool, turned, g)
                    add_bo(i, k, j)
                    if there(g + 1, GROUPS):
                        pool.tensor_copy(dist_s[:, s, :], dist[:, bass.ds((g + 1) * G, G)]).then_inc(dist_staged, 1)
                        gather_src(s)
                else:
                    if there(g + 2, GROUPS):
                        pool.wait_ge(gathered[1 - s], (k + 1) * (16 * 2 * G))
                    add_bo(i, k, j)
                    if there(g + 2, GROUPS):
                        stage(g + 2, 1 - s)
                    if there(g + 1, GROUPS):
                        gather_dst(s)

            steps(pool, step, CHUNKS, CHUNKS // UNROLL - 1)

            pool.wait_ge(masks_made, 1)
            is_unsorted = pool.value_load(unsorted_i[0:1, 0:1])

            def all_pairs(n, values, into, op, empty, count):
                first = n == 0
                dmas = 48 * n + 48 * P * n
                c = count

                def link(ins, at):
                    ins.then_inc(all_step, 1)
                    pool.wait_ge(all_step, at)
                    pool.sem_inc(all_fence, 1)

                link(pool.memset(into, empty), c + 1)
                link(pool.memset(all_count, 0.0) if first else pool.memset(all_less, 0.0), c + 2)
                link(pool.iota(edge_no, pattern=[[1, TILES]], base=0, channel_multiplier=TILES,
                               allow_small_or_imprecise_dtypes=True) if first else pool.memset(all_less, 0.0), c + 3)
                c += 3
                pool.dma_start(scr_rows[:, 0:HEADS, :], heads(values)).then_inc(all_dma, 16)
                pool.dma_start(scr_rows[:, HEADS, :], dst_f[:, :]).then_inc(all_dma, 16)
                pool.dma_start(scr_rows[:, HEADS + 1, :], edge_no).then_inc(all_dma, 16)
                pool.wait_ge(all_dma, dmas + 48)
                dmas += 48
                steps_of = (8 if op == ALU.max else 4) + (4 if first else 0)
                with pool.Fori(0, P) as q:
                    pool.dma_start(heads(all_row), scr_rows[bass.ds(q, 1), 0:HEADS, :]
                                   .to_broadcast([P, HEADS, TILES])).then_inc(all_dma, 16)
                    pool.dma_start(all_dst, scr_rows[bass.ds(q, 1), HEADS, :].to_broadcast([P, TILES]))\
                        .then_inc(all_dma, 16)
                    pool.dma_start(all_idx, scr_rows[bass.ds(q, 1), HEADS + 1, :].to_broadcast([P, TILES]))\
                        .then_inc(all_dma, 16)
                    pool.wait_ge(all_dma, q * 48 + (dmas + 48))
                    pool.sem_inc(all_fence, 1)
                    with pool.Fori(0, TILES) as t:
                        at = [q * (TILES * steps_of) + t * steps_of + c]

                        def one(ins):
                            at[0] = at[0] + 1
                            link(ins, at[0])

                        one(pool.tensor_copy(all_col[:, 0:1], all_dst[:, bass.ds(t, 1)]))
                        one(pool.tensor_scalar(all_mask, dst_f[:, :], all_col[:, 0:1], None, ALU.is_equal))
                        if first:
                            one(pool.tensor_copy(all_col[:, 1:2], all_idx[:, bass.ds(t, 1)]))
                            one(pool.tensor_scalar(all_less, edge_no, all_col[:, 1:2], None, ALU.is_gt))
                            one(pool.tensor_tensor(all_less, all_less, all_mask, ALU.mult))
                            one(pool.tensor_tensor(all_count, all_count, all_less, ALU.add))
                        mask_b = all_mask[:, None, :].to_broadcast([P, HEADS, TILES])
                        value_b = heads(all_row)[:, :, bass.ds(t, 1)].to_broadcast([P, HEADS, TILES])
                        if op == ALU.max:
                            one(pool.tensor_copy(all_col[:, 2:2 + HEADS], heads(all_row)[:, :, bass.ds(t, 1)]
                                                 .rearrange("p h o -> p (h o)")))
                            for h in range(HEADS):
                                ins = pool.tensor_scalar(heads(all_prod)[:, h, :], heads(into)[:, h, :],
                                                         all_col[:, 2 + h:3 + h], None, ALU.max)
                            one(ins)
                            one(pool.tensor_tensor(heads(all_prod), heads(all_prod), mask_b, ALU.mult))
                            one(pool.tensor_scalar(all_mask, all_mask, -1.0, 1.0, ALU.mult, ALU.add))
                            one(pool.tensor_tensor(heads(into), heads(into), mask_b, ALU.mult))
                        else:
                            one(pool.tensor_tensor(heads(all_prod), mask_b, value_b, ALU.mult))
                        one(pool.tensor_tensor(into, into, all_prod, ALU.add))
                c += P * TILES * steps_of
                if first:
                    link(pool.tensor_scalar(rep_f[:, :], all_count, 0.0, None, ALU.is_equal), c + 1)
                    link(pool.tensor_scalar(scat_f[:, :], dst_f[:, :], NO_ROW, None, ALU.subtract), c + 2)
                    link(pool.tensor_tensor(scat_f[:, :], scat_f[:, :], rep_f[:, :], ALU.mult), c + 3)
                    link(pool.tensor_scalar(scat_f[:, :], scat_f[:, :], NO_ROW, None, ALU.add), c + 4)
                    link(pool.tensor_copy(scat_i[:, :], scat_f[:, :]), c + 5)
                    c += 5
                return c

            c = 0
            for n, (op, empty) in enumerate([(ALU.max, -BIG), (ALU.add, 0.0)]):
                pool.wait_ge(fast_done, n + 1)
                with pool.If(is_unsorted):
                    for s in range(2):
                        pool.wait_ge(out_stored[s], CHUNKS // 2 * 16)
                    c = all_pairs(n, scores[:, :, :].rearrange("p h t -> p (h t)"), total, op, empty, c)
                pool.sem_inc(reduced, 1)

            def stage_scat(g, j):
                pool.tensor_copy(scat_stage[:, j, :], scat_i[:, bass.ds(g * G, G)]).then_inc(scat_staged, 1)

            for s in range(2):
                pool.wait_ge(out_stored[s], CHUNKS // 2 * 16)
            stage_scat(0, 0)

            def scatter(g, k, j):
                pool.wait_ge(scat_staged, g + 1)
                pool.wait_ge(rows_ready, g + 1)
                if there(g + 1, GROUPS):
                    after(pool, scattered[(j + 1) % UNROLL], (k if j < 3 else k + 1) * (16 * G))
                    stage_scat(g + 1, (j + 1) % UNROLL)
                for t in range(G):
                    pool.indirect_dma_start(out, bass.IndirectOffsetOnAxis(ap=scat_stage[:, j, t:t + 1], axis=0),
                                            rows_out[:, j, t * D:(t + 1) * D], None,
                                            bounds_check=N_NODES - 1, oob_is_err=False)\
                        .then_inc(scattered[j], 16)

            steps(pool, scatter, GROUPS, GROUPS // UNROLL)
            for j in range(UNROLL):
                pool.wait_ge(scattered[j], len(range(j, GROUPS, UNROLL)) * 16 * G)

        @block.scalar
        def _(act):
            def const(dst, src):
                act.dma_start(dst, src).then_inc(consts_loaded, 16)

            def bcast(name, n):
                return a[name].rearrange("(o n) -> o n", o=1).to_broadcast([P, n])

            for t, name in ((bo_b, "bo"), (gamma_b, "gamma"), (bias_b[:, 0], "beta"), (bias_b[:, 1], "bo"),
                            (bias_b[:, 2], "bv")):
                const(t[:, :], bcast(name, D))
            for t, name in ((Wq, "Wq"), (Wk, "Wk"), (Wv, "Wv"), (Wo, "Wo")):
                const(t[:, :], a[name])
            const(bq[:, :], a["bq"].rearrange("(p o) -> p o", o=1))
            const(bk[:, :], a["bk"].rearrange("(p o) -> p o", o=1))
            for t, name in ((be_b, "be"), (bc2_b, "bc2"), (bd2_b, "bd2")):
                const(t[:, :], bcast(name, HEADS))
            for i in range(G):
                const(bc1[i * CONS_H:(i + 1) * CONS_H, :], a["bc1"].rearrange("(p o) -> p o", o=1))
                const(bd1[i * DIST_H:(i + 1) * DIST_H, :], a["bd1"].rearrange("(p o) -> p o", o=1))
            act.wait_ge(zeroed, 2)
            for i in range(G):
                const(Wc1s[i:i + 1, i * CONS_H:(i + 1) * CONS_H], a["Wc1"])
                const(Wd1s[i:i + 1, i * DIST_H:(i + 1) * DIST_H], a["Wd1"])
                const(Wc2s[i * CONS_H:(i + 1) * CONS_H, i * HEADS:(i + 1) * HEADS], a["Wc2"])
                const(Wd2s[i * DIST_H:(i + 1) * DIST_H, i * HEADS:(i + 1) * HEADS], a["Wd2"])
            for i in range(2):
                const(We2[i * E_DIM:(i + 1) * E_DIM, i * HEADS:(i + 1) * HEADS], a["We"])
            act.wait_ge(consts_loaded, CONST_DMAS * 16)

            def normalise(dst, src, norm, w, rows, done):
                for r in range(rows):
                    last = act.activation(dst[0:w, r * D:(r + 1) * D], src[0:w, r * D:(r + 1) * D], ACT.Identity,
                                          scale=norm[0:w, 0, r:r + 1], bias=norm[0:w, 1, r:r + 1])
                last.then_inc(done, 1)

            def deviation(q, which, rows, c):
                act.wait_ge(var_ready, c + 1)
                act.activation(tmp[:, q, 4, which, 0:rows], tmp[:, q, 3, which, 0:rows], ACT.Sqrt,
                               bias=eps[:, 0:1]).then_inc(std_ready, 1)

            def step(i, k, j):
                g = half(k, j)
                which = joint(i, CHUNKS, 2)
                if there(i - 1, CHUNKS + 2):
                    act.wait_ge(norm_ready, i)
                if there(i - 1, CHUNKS):
                    q = (j - 1) % UNROLL
                    normalise(y[:, q, DVE_ROWS * D:], y[:, q, DVE_ROWS * D:], norm1[:, q % 2, :, DVE_ROWS:],
                              width(i - 1), ROWS - DVE_ROWS, u_ready)
                if there(i - 3, CHUNKS):
                    q = (j - 3) % 2
                    after(act, out_stored[q], (half(k, 0) + (j - 3) // 2) * 16)
                    for c in range(2):
                        normalise(o[:, q, c * 512:(c + 1) * 512], z_ps[q][:, c, :],
                                  norm2[:, q, :, c * G:(c + 1) * G], width(i - 3), G, out_ready)
                if j % 2 == 1 and there(g, GROUPS):
                    act.wait_ge(qk_ready, g + 1)
                    act.activation(qT[:, :], bank_xs, ACT.Identity, bias=bq[:, 0:1]).then_inc(q_kept, 1)
                if which:
                    deviation(j % 2, which, ROWS, i)
                if j % 2 == 0 and there(g, GROUPS):
                    act.wait_ge(turned, g + 1)
                    act.activation(xdT[:, bass.ds(g * GE, GE)], bank_xd, ACT.Copy)
                    act.activation(xsT[:, :], bank_xs, ACT.Copy)
                    act.activation(cdT[:, :], bank_ea[0:G, 2 * P:4 * P], ACT.Copy)
                    after(act, parts_ps, g)
                    act.activation(eaT[:, :], bank_ea[:, 0:2 * P], ACT.Copy).then_inc(turned_kept, 1)
                if j % 2 == 1 and there(g, GROUPS):
                    act.wait_ge(hidden_ps, g + 1)
                    act.activation(h1[:, :], bank_ea[:, 0:P], ACT.Relu, bias=bc1[:, 0:1])
                    act.activation(h2[:, :], bank_ea[0:G * DIST_H, P:2 * P], ACT.Relu, bias=bd1[:, 0:1])\
                        .then_inc(hidden_kept, 1)

            steps(act, step, CHUNKS + 3, CHUNKS // UNROLL - 1)

            act.wait_ge(scores_ready, GROUPS)
            act.activation(cons_all[:, :, :], cons_all[:, :, :], ACT.Sigmoid).then_inc(sig_ready, 1)
            act.wait_ge(shifted, 1)
            flat = scores[:, :, :].rearrange("p h t -> p (h t)")
            act.activation(flat, flat, ACT.Exp).then_inc(exp_ready, 1)

            act.wait_ge(S_ready, 1)

            def step2(s, k, j):
                q = j % 2
                which = joint(s - 3, GROUPS, 2)
                if there(s - 6, GROUPS):
                    act.wait_ge(norm_ready, s + JOINT2)
                    if isinstance(s, int) and s == 6:
                        for slot in range(2):
                            act.wait_ge(out_stored[slot], CHUNKS // 2 * 16)
                    slot = (j - 6) % UNROLL
                    after(act, scattered[slot], (k * 2 + (j - 6) // UNROLL) * (16 * G))
                    normalise(rows_out[:, slot, :], Z_ps[q], norm2[:, 1 - q, :, :], P, G, rows_ready)
                if there(s - 2, GROUPS):
                    act.wait_ge(agg_turned, s - 1)
                    after(act, y2_ready, s - 3)
                    act.activation(aggT[:, q, :], T_ps[q], ACT.Copy).then_inc(aggT_ready, 1)
                if which:
                    deviation(q, which, G, s + JOINT2)
                if there(s, GROUPS):
                    after(act, z2_ready, s - 7)
                    act.activation(xg[:, j, :], xdT[:, bass.ds(s * GE, GE)], ACT.Copy).then_inc(xg_ready, 1)
                if there(s - 3, GROUPS):
                    act.wait_ge(norm_ready, s + JOINT2 + 1)
                    after(act, z2_ready, s - 4)
                    normalise(u[:, 1 - q, :], Y_ps[1 - q], norm1[:, q, :, :], P, G, u2_ready)

            steps(act, step2, GROUPS + 6, GROUPS // SLOTS2, 2, SLOTS2)

        @block.vector
        def _(dve):
            done = [0]

            def link(ins, s=setup_step):
                done[0] += 1
                ins.then_inc(s, 1)
                dve.wait_ge(s, done[0])

            dve.wait_ge(idx_loaded, 80)
            dve.tensor_copy(dst_f[:, :], dst_i[:, :])
            link(dve.tensor_copy(prev_f[:, :], prev_i[:, :]))
            dve.tensor_tensor(unsorted_t[:, :], prev_f[:, :], dst_f[:, :], ALU.is_gt)
            dve.tensor_tensor(same[:, :], prev_f[:, :], dst_f[:, :], ALU.is_equal)
            dve.tensor_scalar(in_first[:, :], dst_f[:, :], dst_f[:, 0:1], None, ALU.is_equal)
            link(dve.tensor_scalar(in_last[:, :], dst_f[:, :], dst_f[:, TILES - 1:TILES], None, ALU.is_equal))
            dve.tensor_reduce(unsorted_p[:, :], unsorted_t[:, :], AX.X, ALU.add)
            dve.tensor_scalar(neg_first[:, :], in_first[:, :], -1.0, BIG, ALU.add, ALU.mult)
            dve.tensor_scalar(neg_last[:, :], in_last[:, :], -1.0, BIG, ALU.add, ALU.mult)
            same_b = same[:, None, :].to_broadcast([P, HEADS, TILES])
            dve.tensor_copy(heads(cont_f)[:, :, 1:TILES], same_b[:, :, 1:TILES])
            dve.memset(heads(cont_f)[:, :, 0:1], 0.0)
            dve.memset(cont[:, HT:HT + 1], 0.0)
            dve.tensor_copy(link8[:, 0, :], same[:, 0:1].to_broadcast([P, HEADS]))
            dve.tensor_copy(link8[:, 1, :], in_first[:, TILES - 1:TILES].to_broadcast([P, HEADS]))
            link(dve.tensor_scalar(rep_f[:, :], same[:, :], -1.0, 1.0, ALU.mult, ALU.add))
            link(dve.scalar_tensor_tensor(scat_f[:, :], dst_f[:, :], -NO_ROW, rep_f[:, :], ALU.add, ALU.mult))
            link(dve.tensor_scalar(scat_f[:, :], scat_f[:, :], NO_ROW, None, ALU.add))
            link(dve.tensor_copy(scat_i[:, :], scat_f[:, :]))
            dve.memset(mul_r[:, :, :], 0.0).then_inc(masks_made_pe, 1)

            dve.wait_ge(consts_loaded, CONST_DMAS * 16)
            dve.wait_ge(ident_made, 7)
            link(dve.tensor_copy(part_bf[:, 0], bias_b))
            link(dve.tensor_tensor(part_f[:, 0], bias_b, part_bf[:, 0], ALU.subtract))
            link(dve.tensor_copy(part_bf[:, 1], part_f[:, 0]))
            link(dve.tensor_tensor(part_f[:, 1], part_f[:, 0], part_bf[:, 1], ALU.subtract))
            link(dve.tensor_copy(part_bf[:, 2], part_f[:, 1]))
            link(dve.tensor_scalar(part_f[:, 0], part_bf[:, 0], ident[:, 0:1], None, ALU.mult))
            link(dve.scalar_tensor_tensor(part_f[:, 1], part_bf[:, 1], ident[:, 1:2], part_f[:, 0],
                                          ALU.mult, ALU.add))
            link(dve.scalar_tensor_tensor(part_f[:, 0], part_bf[:, 2], ident[:, 2:3], part_f[:, 1],
                                          ALU.mult, ALU.add))
            dve.tensor_copy(bias_rows[:, :, :], part_f[:, 0]).then_inc(bias_split, 1)

            dve.wait_ge(links_turned, 1)
            dve.tensor_copy(unsorted_i[:, :], bank_sc[:, 256:257]).then_inc(masks_made, 1)
            link(dve.tensor_copy(link_r[:, :, :], bank_sc[0:HEADS, 0:256].rearrange("p (a b) -> p a b", a=2)))
            linked, whole = link_r[:, 0, :], link_r[:, 1, :]
            dve.tensor_tensor(mul_r[:, 0, 1:P], linked[:, 1:P], whole[:, 0:P - 1], ALU.mult)
            dve.tensor_tensor(mul_r[:, 1, 0:P - 1], linked[:, 1:P], whole[:, 1:P], ALU.mult)
            dve.tensor_copy(mul_r[:, 2, 1:P], linked[:, 1:P])
            link(dve.tensor_copy(mul_r[:, 3, 0:P - 1], linked[:, 1:P]))
            link(dve.tensor_scalar(neg_r[:, :, :], mul_r[:, :, :], -1.0, BIG, ALU.add, ALU.mult))

            def variances(q, which, rows, c, last):
                last.then_inc(stat, 1)
                dve.wait_ge(stat, c * 3 + 1)
                mean_e, mean_o = st[:, q, which, 0:rows, 1], st[:, q, which, 0:rows, 4]
                sq_e, sq_o = st[:, q, which, 0:rows, 2], st[:, q, which, 0:rows, 5]
                two_mean, diff, sq, var = (tmp[:, q, n, which, 0:rows] for n in range(4))
                dve.tensor_tensor(diff, mean_e, mean_o, ALU.subtract)
                dve.tensor_tensor(sq, sq_e, sq_o, ALU.add)
                dve.tensor_tensor(two_mean, mean_e, mean_o, ALU.add).then_inc(stat, 1)
                dve.wait_ge(stat, c * 3 + 2)
                dve.scalar_tensor_tensor(diff, diff, 0.25, diff, ALU.mult, ALU.mult).then_inc(stat, 1)
                dve.wait_ge(stat, c * 3 + 3)
                dve.scalar_tensor_tensor(var, sq, 1.0 / D, diff, ALU.mult, ALU.add).then_inc(var_ready, 1)

            def factors(q, which, rows, c):
                dve.wait_ge(std_ready, c + 1)
                inv, shift = norm[:, q, 0, which, 0:rows], norm[:, q, 1, which, 0:rows]
                dve.reciprocal(inv, tmp[:, q, 4, which, 0:rows]).then_inc(inv_ready, 1)
                dve.wait_ge(inv_ready, c + 1)
                dve.scalar_tensor_tensor(shift, tmp[:, q, 0, which, 0:rows], -0.5, inv, ALU.mult, ALU.mult)\
                   .then_inc(norm_ready, 1)

            def times_gamma(buf, w, rows, done_sem):
                v = buf[0:w, :].rearrange("p (r d) -> p r d", d=D)
                dve.tensor_tensor(v, v, gamma_b[0:w, None, :].to_broadcast([w, rows, D]), ALU.mult)\
                   .then_inc(done_sem, 1)

            def step(i, k, j):
                g = half(k, j)
                q = j % 2
                which = joint(i, CHUNKS, 2)
                if there(i, CHUNKS):
                    dve.wait_ge(y_ready, i + 1)
                    for r in range(ROWS):
                        last = dve.bn_stats(st[0:width(i), q, 0, r, :], y[0:width(i), j, r * D:(r + 1) * D])
                if there(i - 1, CHUNKS):
                    dve.wait_ge(rows_normed, i)
                    dve.wait_ge(u_ready, i)
                    times_gamma(y[:, (j - 1) % UNROLL, :], width(i - 1), ROWS, ug_ready)
                if there(i - 2, CHUNKS):
                    dve.wait_ge(z_ready, i - 1)
                    w = width(i - 2)
                    for r in range(ROWS):
                        last = dve.bn_stats(st[0:w, q, 1, r, :], z_ps[q][0:w, r // G, r % G * D:(r % G + 1) * D])
                if which:
                    variances(q, which, ROWS, i, last)
                if j % 2 == 1 and there(g, GROUPS):
                    dve.wait_ge(q_kept, g + 1)
                    dve.scalar_tensor_tensor(prod[:, :], bank_xd, bk[:, 0:1], qT[:, :], ALU.add, ALU.mult)\
                       .then_inc(prod_ready, 1)
                if j % 2 == 0 and there(g - 1, GROUPS):
                    dve.wait_ge(parts_ps, g)
                    for n, (dst, bias) in enumerate(((scores, be_b), (cons_all, bc2_b), (dist_all, bd2_b))):
                        last = dve.tensor_tensor(
                            dst[:, :, bass.ds(g * G - G, G)],
                            bank_sc[:, n * G * HEADS:(n + 1) * G * HEADS].rearrange("p (t h) -> p h t", h=HEADS),
                            bias[:, :, None].to_broadcast([P, HEADS, G]), ALU.add)
                    last.then_inc(scores_ready, 1)
                if which:
                    factors(q, which, ROWS, i)
                if there(i, CHUNKS):
                    dve.wait_ge(norm_ready, i + 1)
                    w = width(i)
                    for r in range(DVE_ROWS):
                        row = y[0:w, j, r * D:(r + 1) * D]
                        last = dve.tensor_scalar(row, row, norm1[0:w, q, 0, r:r + 1], norm1[0:w, q, 1, r:r + 1],
                                                 ALU.mult, ALU.add)
                    last.then_inc(rows_normed, 1)

            steps(dve, step, CHUNKS + 2, CHUNKS // UNROLL - 1)

            dve.wait_ge(sig_ready, 1)
            done[0] = 0
            link(dve.tensor_tensor(scores[:, :, :], scores[:, :, :], cons_all[:, :, :], ALU.mult), soft_step)
            link(dve.tensor_tensor(scores[:, :, :], scores[:, :, :], dist_all[:, :, :], ALU.add), soft_step)

            flat = scores[:, :, :].rearrange("p h t -> p (h t)")

            def soft(ins):
                link(ins, soft_step)

            def segments(n, first_mask, op0, op, start, masks_r, comb0, in_masks):
                soft(dve.tensor_tensor_scan(run, first_mask, flat, start, op0, op))
                soft(dve.scalar_tensor_tensor(ends, cont_b, 0.0, run, ALU.is_equal, ALU.mult))
                soft(dve.tensor_tensor_scan(total[:, ::-1], cont_b[:, ::-1], ends[:, ::-1], 0.0,
                                            ALU.mult, ALU.add))
                dve.sem_inc(edges_out, 1)
                dve.wait_ge(edges_turned, n + 1)
                first_r, last_r = bank_sc[0:HEADS, 0:P], bank_sc[0:HEADS, P:2 * P]
                dve.tensor_tensor(edge_r[:, 0, 1:P], last_r[:, 0:P - 1], masks_r[:, 2, 1:P], comb0)
                dve.tensor_tensor(edge_r[:, 1, 0:P - 1], first_r[:, 1:P], masks_r[:, 3, 0:P - 1], comb0)
                dve.memset(edge_r[:, 0, 0:1], start)
                soft(dve.memset(edge_r[:, 1, P - 1:P], start))
                dve.tensor_tensor_scan(carry_r[:, 0, :], masks_r[:, 0, :], edge_r[:, 0, :], start, op0, op)
                dve.tensor_tensor_scan(carry_r[:, 1, ::-1], masks_r[:, 1, ::-1], edge_r[:, 1, ::-1], start, op0, op)\
                   .then_inc(carries_out, 1)
                dve.wait_ge(carries_turned, n + 1)
                soft(dve.tensor_copy(carry[:, :, :], bank_sc[:, 256:256 + 2 * HEADS]
                                     .rearrange("p (a b) -> p a b", a=2)))
                th = heads(total)
                for side in range(2):
                    for h in range(HEADS):
                        last = dve.scalar_tensor_tensor(th[:, h, :], in_masks[side][:, :], carry[:, side, h:h + 1],
                                                        th[:, h, :], comb0, op)
                    soft(last)
                dve.sem_inc(fast_done, 1)
                dve.wait_ge(reduced, n + 1)

            soft(dve.tensor_scalar(neg_f, cont_f, -1.0, BIG, ALU.add, ALU.mult))
            segments(0, neg_f, ALU.add, ALU.max, -BIG, neg_r, ALU.add, (neg_first, neg_last))
            dve.tensor_tensor(flat, flat, total, ALU.subtract).then_inc(shifted, 1)
            dve.wait_ge(exp_ready, 1)
            segments(1, cont_f, ALU.mult, ALU.add, 0.0, mul_r, ALU.mult, (in_first, in_last))
            soft(dve.reciprocal(run, total))
            dve.tensor_tensor(flat, total, run, ALU.mult).then_inc(S_ready, 1)
            dve.wait_ge(S_ready, 1)

            def step2(s, k, j):
                q = j % 2
                which = joint(s - 3, GROUPS, 2)
                if there(s - 4, GROUPS):
                    dve.wait_ge(u2_ready, s - 3)
                    times_gamma(u[:, q, :], P, G, ug2_ready)
                if there(s - 3, GROUPS):
                    dve.wait_ge(y2_ready, s - 2)
                    for r in range(G):
                        last = dve.bn_stats(st[:, q, 0, r, :], Y_ps[1 - q][:, r * D:(r + 1) * D])
                if there(s - 5, GROUPS):
                    dve.wait_ge(z2_ready, s - 4)
                    for r in range(G):
                        last = dve.bn_stats(st[:, q, 1, r, :], Z_ps[1 - q][:, r * D:(r + 1) * D])
                if which:
                    variances(q, which, G, s + JOINT2, last)
                    factors(q, which, G, s + JOINT2)
                if there(s - 1, GROUPS):
                    dve.wait_ge(v_ready, s)
                    after(dve, agg_turned, s - 2)
                    S = scores[:, :, bass.ds((s - 1) * G, G)].rearrange("p h t -> p t h")
                    dve.tensor_tensor(agg[:, 1 - q, :].rearrange("p (t h d) -> p t h d", t=G, h=HEADS),
                                      V_ps[1 - q].rearrange("p (t h d) -> p t h d", t=G, h=HEADS),
                                      S[:, :, :, None].to_broadcast([P, G, HEADS, HEAD_DIM]), ALU.mult)\
                       .then_inc(agg_ready, 1)

            steps(dve, step2, GROUPS + 5, GROUPS // SLOTS2, 1, SLOTS2)

        @block.tensor
        def _(pe):
            pe.wait_ge(ident_made, 7)
            pe.wait_ge(masks_made_pe, 1)
            pe.transpose(bank_sc[0:HEADS, 0:P], link8[:, 0, :], ident[:, :])
            pe.transpose(bank_sc[0:HEADS, P:2 * P], link8[:, 1, :], ident[:, :])
            pe.matmul(bank_sc[:, 256:257], ones[:, :], unsorted_p[:, :], start=True, stop=True)\
              .then_inc(links_turned, 1)
            pe.wait_ge(consts_loaded, CONST_DMAS * 16)
            pe.wait_ge(bias_split, 1)
            pe.wait_ge(masks_made, 1)

            def by_tile(bank):
                return bank.rearrange("p (t d) -> p t d", d=D)

            def dense_z(i, j):
                w = width(i)
                s = j % 2
                pe.wait_ge(ug_ready, i + 1)
                for c in range(2):
                    after(pe, out_ready, 2 * i - 3 + c)
                    cols = slice(c * 512, (c + 1) * 512)
                    pe.matmul(by_tile(z_ps[s][0:w, c, :]), ones_bf[:, 0:w], beta_rows,
                              start=True, stop=False)
                    pe.matmul(z_ps[s][0:w, c, :], ident[0:w, 0:w], x_in[0:w, j, cols], start=False, stop=False)
                    last = pe.matmul(z_ps[s][0:w, c, :], ident[0:w, 0:w], y[0:w, j, cols], start=False, stop=True)
                last.then_inc(z_ready, 1)

            def step(i, k, j):
                g = half(k, j)
                s = j // 2
                if j % 2 == 0 and there(g - 1, GROUPS):
                    pe.wait_ge(prod_ready, g)
                    pe.wait_ge(hidden_kept, g)
                    after(pe, scores_ready, g - 1)
                    for t in range(2):
                        pe.matmul(bank_sc[:, t * 2 * HEADS:(t + 1) * 2 * HEADS], eaT[:, t * P:(t + 1) * P], We2[:, :],
                                  start=True, stop=False)
                        for c in range(2):
                            pe.matmul(bank_sc[:, t * 2 * HEADS:(t + 1) * 2 * HEADS],
                                      prod[:, (2 * t + c) * P:(2 * t + c + 1) * P],
                                      head_sel3[:, (1 - c) * HEADS:(3 - c) * HEADS], start=False, stop=c == 1)
                    pe.matmul(bank_sc[:, G * HEADS:2 * G * HEADS], h1[:, :], Wc2s[:, :], start=True, stop=True)
                    pe.matmul(bank_sc[:, 2 * G * HEADS:3 * G * HEADS], h2[:, :], Wd2s[:, :], start=True, stop=True)\
                      .then_inc(parts_ps, 1)
                if j % 2 == 0 and there(g, GROUPS):
                    pe.wait_ge(gathered[s], (k + 1) * (16 * 2 * G))
                    pe.wait_ge(ea_loaded[s], (k + 1) * 16)
                    pe.wait_ge(dist_staged, g + 1)
                    after(pe, q_kept, g)
                    after(pe, prod_ready, g)
                    after(pe, hidden_kept, g)
                    for t in range(G):
                        pe.transpose(bank_xd[:, t * P:(t + 1) * P], xd[:, s, t, 0:D], ident[:, :])
                    for t in range(G):
                        pe.transpose(bank_xs[:, t * P:(t + 1) * P], xs[:, s, t, :], ident[:, :])
                    for t in range(2):
                        pe.transpose(bank_ea[:, t * P:(t + 1) * P], ea[:, s, t * P:(t + 1) * P], ident[:, :])
                    pe.transpose(bank_ea[0:G, 2 * P:3 * P], xd[:, s, :, D], ident[:, :])
                    pe.transpose(bank_ea[0:G, 3 * P:4 * P], dist_s[:, s, :], ident[:, :])\
                      .then_inc(turned, 1)
                if j % 2 == 1 and there(g, GROUPS):
                    pe.wait_ge(turned_kept, g + 1)
                    pe.matmul(bank_xs, Wq[:, :], xsT[:, :], start=True, stop=True)
                    pe.matmul(bank_xd, Wk[:, :], xdT[:, bass.ds(g * GE, GE)], start=True, stop=True)\
                      .then_inc(qk_ready, 1)
                    pe.matmul(bank_ea[:, 0:P], Wc1s[:, :], cdT[:, 0:P], start=True, stop=True)
                    pe.matmul(bank_ea[0:G * DIST_H, P:2 * P], Wd1s[:, :], cdT[:, P:2 * P], start=True, stop=True)\
                      .then_inc(hidden_ps, 1)
                if there(i - 1, CHUNKS):
                    dense_z(i - 1, (j - 1) % UNROLL)

            steps(pe, step, CHUNKS + 1, CHUNKS // UNROLL - 1)

            th = heads(total)
            for n in range(2):
                pe.wait_ge(edges_out, n + 1)
                pe.transpose(bank_sc[0:HEADS, 0:P], th[:, :, 0], ident[:, :])
                pe.transpose(bank_sc[0:HEADS, P:2 * P], th[:, :, TILES - 1], ident[:, :]).then_inc(edges_turned, 1)
                pe.wait_ge(carries_out, n + 1)
                for side in range(2):
                    last = pe.transpose(bank_sc[:, 256 + side * HEADS:256 + (side + 1) * HEADS], carry_r[:, side, :],
                                        ident[0:HEADS, 0:HEADS])
                last.then_inc(carries_turned, 1)

            def add_bias(into, rows, stop):
                return pe.matmul(by_tile(into), ones_bf[:, :], rows, start=False, stop=stop, skip_group_check=True)

            def product(into, turned_rows, weights, first):
                for t in range(G):
                    pe.matmul(into[:, t * P:(t + 1) * P], turned_rows[:, t * P:(t + 1) * P], weights,
                              start=first and t == 0, stop=False, skip_group_check=True)

            def step2(s, k, j):
                q = j % 2
                if there(s - 2, GROUPS):
                    pe.wait_ge(agg_ready, s - 1)
                    after(pe, aggT_ready, s - 3)
                    for t in range(G):
                        last = pe.transpose(T_ps[q][:, t * P:(t + 1) * P], agg[:, q, t * P:(t + 1) * P], ident[:, :])
                    last.then_inc(agg_turned, 1)
                if there(s - 1, GROUPS):
                    pe.wait_ge(xg_ready, s)
                    after(pe, agg_ready, s - 2)
                    product(V_ps[1 - q], xg[:, (j - 1) % SLOTS2, :], Wv[:, :], True)
                    add_bias(V_ps[1 - q], bv_rows, True).then_inc(v_ready, 1)
                if there(s - 4, GROUPS):
                    pe.wait_ge(ug2_ready, s - 3)
                    after(pe, rows_ready, s - 5)
                    product(Z_ps[q], xg[:, (j - 4) % SLOTS2, :], ident[:, :], True)
                    add_bias(Z_ps[q], beta_rows, False)
                    pe.matmul(Z_ps[q], ident[:, :], u[:, q, :], start=False, stop=True,
                              skip_group_check=True).then_inc(z2_ready, 1)
                if there(s - 2, GROUPS):
                    pe.wait_ge(aggT_ready, s - 1)
                    after(pe, u2_ready, s - 3)
                    product(Y_ps[q], xg[:, (j - 2) % SLOTS2, :], ident[:, :], True)
                    product(Y_ps[q], aggT[:, q, :], Wo[:, :], False)
                    add_bias(Y_ps[q], bo_rows, True).then_inc(y2_ready, 1)

            steps(pe, step2, GROUPS + 4, GROUPS // SLOTS2, 1, SLOTS2)


_WEIGHTS = ["Wq", "bq", "Wk", "bk", "Wv", "bv", "We", "be", "Wc1", "bc1", "Wc2", "bc2", "Wd1", "bd1", "Wd2", "bd2",
            "Wo", "bo", "gamma", "beta"]
CONST_DMAS = 5 + 4 + 2 + 3 + 2 * G + 4 * G + 2


def kernel(**inputs):
    import numpy as _np
    import concourse.bacc as _bacc
    from concourse import mybir as _mybir
    from concourse.bass_utils import run_bass_kernel_spmd as _run

    nc = _bacc.Bacc("TRN2", target_bir_lowering=False, num_devices=1)
    pad = PAD_EDGES - N_EDGES

    def padded(v, fill):
        tail = _np.full((pad,) + v.shape[1:], fill, v.dtype)
        return _np.concatenate([v, tail])

    x = _np.asarray(inputs["x"])
    xn = _np.concatenate([x, _np.asarray(inputs["node_vec1"])], axis=1)
    xn = _np.concatenate([xn, _np.zeros((1, XN), x.dtype)])
    data = {
        "x": x, "xn": xn,
        "src": padded(_np.asarray(inputs["src"]), 0),
        "dst": padded(_np.asarray(inputs["dst"]), N_NODES),
        "edge_attr": padded(_np.asarray(inputs["edge_attr_64"]), 0),
        "edge_weight": padded(_np.asarray(inputs["edge_weight1"]).reshape(-1), 0),
    }
    for name in _WEIGHTS:
        data[name] = _np.asarray(inputs["L0_gnn_" + name])
    arrays, args = {}, {}
    for name, v in data.items():
        v = _np.ascontiguousarray(v)
        arrays[f"in_{name}_dram"] = v
        args[name] = nc.dram_tensor(f"in_{name}_dram", v.shape, _mybir.dt.from_np(v.dtype), kind="ExternalInput").ap()
    out = nc.dram_tensor("out_0_dram", (N_NODES, D), _mybir.dt.float32, kind="ExternalOutput").ap()
    gnn_kernel(nc, args, out)
    r = _run(nc, [arrays], core_ids=[0])
    return r.results[0]["out_0_dram"]
```

```python
from contextlib import ExitStack

import concourse.bass as bass
from concourse import mybir

F32 = mybir.dt.float32
BF16 = mybir.dt.bfloat16
I32 = mybir.dt.int32
ALU = mybir.AluOpType
ACT = mybir.ActivationFunctionType
AX = mybir.AxisListType

P = 128
N_NODES = 100000
D = 128
E_DIM = 64
HEADS = 8
HEAD_DIM = D // HEADS
CONS_H = 32
DIST_H = 16
N_EDGES = 25000
TILES = -(-N_EDGES // P)
PAD_EDGES = P * TILES
G = 4
GROUPS = TILES // G
GE = G * P
XN = D + 1
ROWS = 8
DVE_ROWS = (2, 2)
POOL_ROWS = 7
CW = ROWS * D
CHUNK = P * ROWS
FULL_CHUNKS = N_NODES // CHUNK
REST_P = (N_NODES - FULL_CHUNKS * CHUNK) // ROWS
CHUNKS = FULL_CHUNKS + 1
UNROLL = 4
XG_EARLY = 4
SLOTS2 = 8
PEELED = 2
JOINT2 = CHUNKS + 2 - 3
S_PARTS = [0, 2, 14, 22, 29, 35, 40, 45, GROUPS]
EPS = 1e-5
BIG = 3e38
NO_ROW = 131072.0

CONSTS, CONST_COLS = {}, 0
for _name, _rows, _cols in (
        ("Wq", D, D), ("Wk", D, D), ("Wv", D, D), ("Wo", D, D), ("bq", D, 1), ("bk", D, 1),
        ("We2", 2 * E_DIM, 2 * HEADS), ("Wc1s", G, G * CONS_H), ("Wd1s", G, G * DIST_H),
        ("Wc2s", G * CONS_H, G * HEADS), ("Wd2s", G * DIST_H, G * HEADS), ("bc1s", G * CONS_H, 1),
        ("bd1s", G * DIST_H, 1), ("be", P, HEADS), ("bc2", P, HEADS), ("bd2", P, HEADS), ("gamma", P, D),
        ("bo", P, D)):
    CONSTS[_name] = (_rows, _cols, CONST_COLS)
    CONST_COLS += _cols
assert TILES % G == 0 and REST_P * ROWS + FULL_CHUNKS * CHUNK == N_NODES
assert CHUNKS == 2 * GROUPS and GROUPS == 12 * UNROLL + 1 and E_DIM * 2 == P


def after(engine, sem, count):
    if not isinstance(count, int) or count > 0:
        engine.wait_ge(sem, count)


def gnn_kernel(nc, a, out):
    ctx = ExitStack()
    with ctx:
        def sb(name, shape, dt=F32):
            return ctx.enter_context(nc.sbuf_tensor(name, shape, dt))

        def sem(name):
            return ctx.enter_context(nc.semaphore(name))

        ident = sb("ident", [P, P])
        eps = sb("eps", [P, 1])
        ones = sb("ones", [P, P])
        ones_bf = sb("ones_bf", [P, P], BF16)
        consts = sb("consts", [P, CONST_COLS])

        def const(name):
            rows, cols, at = CONSTS[name]
            return consts[0:rows, at:at + cols]

        Wq, Wk, Wv, Wo = (const(n) for n in ("Wq", "Wk", "Wv", "Wo"))
        bq, bk = const("bq"), const("bk")
        head_sel3 = sb("head_sel3", [P, 3 * HEADS])
        head_sel = head_sel3[:, HEADS:2 * HEADS]
        We2 = const("We2")
        Wc1s, Wd1s = const("Wc1s"), const("Wd1s")
        Wc2s, Wd2s = const("Wc2s"), const("Wd2s")
        bc1, bd1 = const("bc1s"), const("bd1s")
        be_b, bc2_b, bd2_b = const("be"), const("bc2"), const("bd2")
        gamma_b, bo_b = const("gamma"), const("bo")
        bias_rows = sb("bias_rows", [P, 3, D], BF16)
        beta_rows, bo_rows, bv_rows = (bias_rows[:, n:n + 1, :].to_broadcast([P, G, D]) for n in range(3))
        ends_i = sb("ends_i", [P, 2, TILES], I32)
        src_i, dst_i = ends_i[:, 0, :], ends_i[:, 1, :]
        dist = sb("dist", [P, TILES])
        dst_f = sb("dst_f", [P, TILES])
        unsorted_p = sb("unsorted_p", [P, 1])
        unsorted_i = sb("unsorted_i", [P, 1], I32)
        same = sb("same", [P, TILES])
        cont = sb("cont", [P, HEADS * TILES + 1])
        in_first = sb("in_first", [P, TILES])
        in_last = sb("in_last", [P, TILES])
        neg_first = sb("neg_first", [P, TILES])
        neg_last = sb("neg_last", [P, TILES])
        link8 = sb("link8", [P, 2, HEADS])
        link_r = sb("link_r", [HEADS, 2, P])
        mul_r = sb("mul_r", [HEADS, 4, P])
        neg_r = sb("neg_r", [HEADS, 4, P])
        edge_r = sb("edge_r", [HEADS, 2, P])
        carry_r = sb("carry_r", [HEADS, 2, P])
        carry = sb("carry", [P, 2, HEADS])
        rep_f = sb("rep_f", [P, TILES])
        scat_f = sb("scat_f", [P, TILES])
        scat_i = sb("scat_i", [P, TILES], I32)
        x_in = sb("x_in", [P, UNROLL, CW])
        y = sb("y", [P, UNROLL, CW])
        o = sb("o", [P, 2, CW])
        st = sb("st", [P, 2, 2, ROWS, 6])
        tmp = sb("tmp", [P, 2, 5, 2, ROWS])
        norm = sb("norm", [P, 2, 2, 2, ROWS])
        xs = sb("xs", [P, 2, G, D])
        xd = sb("xd", [P, 2, G, XN])
        norm1, norm2 = norm[:, :, :, 0], norm[:, :, :, 1]
        idx = sb("idx", [P, 2, 2, G], I32)
        dist_s = sb("dist_s", [P, 2, G])
        ea = sb("ea", [P, 2, G * E_DIM])
        xsT = sb("xsT", [P, GE])
        xdT = sb("xdT", [P, TILES * P])
        eaT = sb("eaT", [P, 2 * P])
        cdT = sb("cdT", [G, 2 * P])
        qT = sb("qT", [P, GE])
        prod = sb("prod", [P, GE])
        h1 = sb("h1", [G * CONS_H, P])
        h2 = sb("h2", [G * DIST_H, P])
        cons_all = sb("cons_all", [P, HEADS, TILES])
        dist_all = sb("dist_all", [P, HEADS, TILES])
        scores = sb("scores", [P, HEADS, TILES])
        scat_stage = sb("scat_stage", [P, UNROLL, G], I32)

        x_flat = x_in[:, :, :].rearrange("p a b -> p (a b)")
        y_flat = y[:, :, :].rearrange("p a b -> p (a b)")
        o_flat = o[:, :, :].rearrange("p a b -> p (a b)")
        HT = HEADS * TILES
        cont_f = cont[:, 0:HT]
        cont_b = cont[:, 1:HT + 1]
        early = xdT[:, TILES * P - 2560:TILES * P]
        bias_b = early[:, 0:3 * D].rearrange("p (n d) -> p n d", n=3)
        part_f = early[:, 3 * D:9 * D].rearrange("p (s n d) -> p s n d", s=2, n=3)
        part_bf = early[:, 9 * D:15 * D].bitcast(BF16)[:, 0:9 * D] \
            .rearrange("p (s n d) -> p s n d", s=3, n=3)
        prev_f = early[:, 15 * D:15 * D + TILES]
        unsorted_t = early[:, 15 * D + 2 * TILES:15 * D + 3 * TILES]
        prev_i = early[:, 15 * D + TILES:15 * D + 2 * TILES].bitcast(I32)

        def heads(ap):
            return ap.rearrange("p (h t) -> p h t", h=HEADS)

        run = x_flat[:, UNROLL * CW - HT:]
        th_all = cons_all[:, :, :]
        total = th_all.rearrange("p h t -> p (h t)")
        neg = y_flat[:, 0:HT + 1]
        neg_f, neg_b = neg[:, 0:HT], neg[:, 1:HT + 1]
        all_row = y_flat[:, HT:2 * HT]
        all_prod = o_flat[:, 0:HT]
        all_dst = x_flat[:, 2 * HT:2 * HT + TILES]
        all_mask = x_flat[:, 2 * HT + TILES:2 * HT + 2 * TILES]
        all_idx = x_flat[:, 2 * HT + 2 * TILES:2 * HT + 3 * TILES]
        all_less = x_flat[:, 2 * HT + 3 * TILES:2 * HT + 4 * TILES]
        edge_no = o_flat[:, HT:HT + TILES]
        all_count = y_flat[:, 2 * HT:2 * HT + TILES]
        all_col = y_flat[:, 2 * HT + TILES:2 * HT + TILES + 2 + HEADS]
        xg = x_flat.rearrange("p (s n) -> p s n", s=SLOTS2)
        agg, aggT, u = (y_flat[:, 2 * n * GE:2 * (n + 1) * GE].rearrange("p (s n) -> p s n", s=2)
                        for n in range(3))
        rows_out = o_flat.rearrange("p (s n) -> p s n", s=UNROLL)

        scr_rows = nc.dram_tensor("scr_rows", [P, HEADS + 2, TILES], F32).ap()

        banks = [ctx.enter_context(nc.psum_tensor(f"bank{i}", [P, 2, 512], F32)) for i in range(4)]
        z_ps = [banks[0][:, :, :], banks[1][:, :, :]]
        bank_xs = banks[2][:, 0, :]
        bank_xd = banks[2][:, 1, :]
        bank_ea = banks[3][:, 0, :]
        bank_sc = banks[3][:, 1, :]
        V_ps, T_ps, Y_ps, XB_ps = ([bank[:, s, :] for s in range(2)] for bank in banks)

        ident_made = sem("ident_made")
        idx_loaded = sem("idx_loaded")
        consts_loaded = sem("consts_loaded")
        masks_made = sem("masks_made")
        links_turned = sem("links_turned")
        bias_split = sem("bias_split")
        masks_made_pe = sem("masks_made_pe")
        setup_step = sem("setup_step")
        x_loaded = [sem(f"x_loaded{j}") for j in range(UNROLL)]
        y_ready = sem("y_ready")
        own_y = sem("own_y")
        stat = sem("stat")
        var_ready = sem("var_ready")
        std_ready = sem("std_ready")
        inv_ready = sem("inv_ready")
        norm_ready = sem("norm_ready")
        rows_normed = sem("rows_normed")
        u_ready = sem("u_ready")
        ug_ready = sem("ug_ready")
        x_used = sem("x_used")
        z_ready = sem("z_ready")
        out_ready = sem("out_ready")
        out_stored = [sem(f"out_stored{j}") for j in range(2)]
        idx_staged = sem("idx_staged")
        dist_staged = sem("dist_staged")
        gathered = [sem(f"gathered{j}") for j in range(2)]
        ea_loaded = [sem(f"ea_loaded{j}") for j in range(2)]
        turned = sem("turned")
        turned_kept = sem("turned_kept")
        qk_ready = sem("qk_ready")
        hidden_ps = sem("hidden_ps")
        q_kept = sem("q_kept")
        hidden_kept = sem("hidden_kept")
        prod_ready = sem("prod_ready")
        parts_ps = sem("parts_ps")
        sig_ready = sem("sig_ready")
        scores_ready = sem("scores_ready")
        soft_step = sem("soft_step")
        edges_out = sem("edges_out")
        edges_turned = sem("edges_turned")
        carries_out = sem("carries_out")
        carries_turned = sem("carries_turned")
        fast_done = sem("fast_done")
        reduced = sem("reduced")
        shifted = sem("shifted")
        exp_ready = sem("exp_ready")
        all_dma = sem("all_dma")
        all_step = sem("all_step")
        all_fence = sem("all_fence")
        
        S_ready = sem("S_ready")
        xg_ready = sem("xg_ready")
        xb_ready = sem("xb_ready")
        v_ready = sem("v_ready")
        agg_turned = sem("agg_turned")
        aggT_ready = sem("aggT_ready")
        agg_ready = sem("agg_ready")
        y2_ready = sem("y2_ready")
        u2_ready = sem("u2_ready")
        ug2_ready = sem("ug2_ready")
        z2_ready = sem("z2_ready")
        rows_ready = sem("rows_ready")
        scat_staged = sem("scat_staged")
        scattered = [sem(f"scattered{j}") for j in range(UNROLL)]

        def width(i):
            return REST_P if isinstance(i, int) and i == CHUNKS - 1 else P

        def chunk_rows(t, i):
            w = width(i)
            return t[bass.ds(i * CHUNK, w * ROWS), :].rearrange("(p r) d -> p (r d)", r=ROWS)

        def x_free(i):
            return i - UNROLL + 1

        def steps(engine, step, last, whole, peeled=PEELED, unroll=UNROLL):
            for i in range(peeled * unroll):
                step(i, i // unroll, i % unroll)
            with engine.Fori(peeled, whole) as k:
                for j in range(unroll):
                    step(k * unroll + j, k, j)
            for i in range(whole * unroll, last):
                step(i, i // unroll, i % unroll)

        def there(i, n):
            return not isinstance(i, int) or 0 <= i < n

        def joint(i, n, lag):
            first, second = there(i, n), there(i - lag, n)
            return slice(0 if first else 1, 2 if second else 1) if first or second else None

        def half(k, j):
            return k * (UNROLL // 2) + j // 2

        ea_v = a["edge_attr"].rearrange("(p t) f -> p (t f)", t=TILES)

        block = ctx.enter_context(nc.Block())

        @block.sync
        def _(sp):
            after_none = a["dst"]
            for into, first in ((dst_i, 1), (prev_i, 0)):
                sp.dma_start(into, after_none[first:first + PAD_EDGES].rearrange("(p t) -> p t", t=TILES))\
                  .then_inc(idx_loaded, 16)
            sp.dma_start(src_i, a["src"].rearrange("(p t) -> p t", t=TILES)).then_inc(idx_loaded, 16)
            sp.dma_start(dist[:, :], a["edge_weight"].rearrange("(p t) -> p t", t=TILES)).then_inc(idx_loaded, 16)

            def load_x(i, k, j):
                after(sp, x_used, x_free(i))
                w = width(i)
                sp.dma_start(x_in[0:w, j, :], chunk_rows(a["x"], i)).then_inc(x_loaded[j], 16)

            def load_ea(g, s):
                after(sp, turned, g - 1)
                sp.dma_start(ea[:, s, :], ea_v[:, bass.ds(g * (G * E_DIM), G * E_DIM)]).then_inc(ea_loaded[s], 16)

            load_x(0, 0, 0)
            load_ea(0, 0)
            load_x(1, 0, 1)

            def step(i, k, j):
                g = half(k, j)
                if there(i + 2, CHUNKS):
                    load_x(i + 2, k if j < 2 else k + 1, (j + 2) % UNROLL)
                if j % 2 == 0 and there(g + 1, GROUPS):
                    load_ea(g + 1, (j // 2 + 1) % 2)
                if there(i - 3, CHUNKS):
                    sp.wait_ge(out_ready, 2 * i - 4)
                    w = width(i - 3)
                    q = (j - 3) % 2
                    sp.dma_start(chunk_rows(out, i - 3), o[0:w, q, :]).then_inc(out_stored[q], 16)

            steps(sp, step, CHUNKS + 3, CHUNKS // UNROLL - 1)

        @block.gpsimd
        def _(pool):
            pool.memset(ident[:, :], 0.0).then_inc(ident_made, 1)
            pool.memset(head_sel3[:, :], 0.0).then_inc(ident_made, 1)
            pool.wait_ge(ident_made, 2)
            pool.memset(head_sel, float(HEAD_DIM) ** -0.5).then_inc(ident_made, 1)
            pool.wait_ge(ident_made, 3)
            pool.affine_select(out=ident[:, :], in_=ident[:, :], compare_op=ALU.not_equal, fill=1.0,
                               base=0, pattern=[[-1, P]], channel_multiplier=1).then_inc(ident_made, 1)
            pool.affine_select(out=head_sel, in_=head_sel, compare_op=ALU.is_ge, fill=0.0,
                               base=0, pattern=[[-HEAD_DIM, HEADS]], channel_multiplier=1).then_inc(ident_made, 1)
            pool.wait_ge(ident_made, 5)
            pool.affine_select(out=head_sel, in_=head_sel, compare_op=ALU.is_ge, fill=0.0,
                               base=HEAD_DIM - 1, pattern=[[HEAD_DIM, HEADS]], channel_multiplier=-1)\
                .then_inc(ident_made, 1)
            pool.memset(ones[:, :], 1.0)
            pool.memset(eps[:, :], EPS)
            pool.memset(ones_bf[:, :], 1.0).then_inc(ident_made, 1)

            def stage(g, s):
                pool.tensor_copy(idx[:, s, :, :], ends_i[:, :, bass.ds(g * G, G)]).then_inc(idx_staged, 1)

            def gather_src(s):
                for t in range(G):
                    pool.indirect_dma_start(xs[:, s, t, :], None, a["x"],
                                            bass.IndirectOffsetOnAxis(ap=idx[:, s, 0, t:t + 1], axis=0))\
                        .then_inc(gathered[s], 16)

            def gather_dst(s):
                for t in range(G):
                    pool.indirect_dma_start(xd[:, s, t, :], None, a["xn"],
                                            bass.IndirectOffsetOnAxis(ap=idx[:, s, 1, t:t + 1], axis=0))\
                        .then_inc(gathered[s], 16)

            def add_bo(i, k, j):
                pool.wait_ge(x_loaded[j], k * 16 + 16)
                after(pool, z_ready, 2 * x_free(i))
                w = width(i)
                pool.tensor_tensor(
                    y[0:w, j, 0:POOL_ROWS * D].rearrange("p (r d) -> p r d", d=D),
                    x_in[0:w, j, 0:POOL_ROWS * D].rearrange("p (r d) -> p r d", d=D),
                    bo_b[0:w, None, :].to_broadcast([w, POOL_ROWS, D]), ALU.add).then_inc(y_ready, 1)

            pool.wait_ge(idx_loaded, 64)
            stage(0, 0)
            stage(1, 1)
            pool.tensor_copy(dist_s[:, 0, :], dist[:, 0:G]).then_inc(dist_staged, 1)
            pool.wait_ge(idx_staged, 2)
            gather_src(0)
            gather_dst(0)
            pool.wait_ge(consts_loaded, 32)

            def step(i, k, j):
                g = half(k, j)
                s = (j // 2 + 1) % 2
                if j % 2 == 0:
                    if there(g + 1, GROUPS):
                        pool.wait_ge(idx_staged, g + 2)
                        after(pool, turned, g)
                    add_bo(i, k, j)
                    if there(g + 1, GROUPS):
                        pool.tensor_copy(dist_s[:, s, :], dist[:, bass.ds((g + 1) * G, G)]).then_inc(dist_staged, 1)
                        gather_src(s)
                else:
                    if there(g + 2, GROUPS):
                        pool.wait_ge(gathered[1 - s], (k + 1) * (16 * 2 * G))
                    add_bo(i, k, j)
                    if there(g + 2, GROUPS):
                        stage(g + 2, 1 - s)
                    if there(g + 1, GROUPS):
                        gather_dst(s)

            steps(pool, step, CHUNKS, CHUNKS // UNROLL - 1)

            pool.wait_ge(masks_made, 1)
            is_unsorted = pool.value_load(unsorted_i[0:1, 0:1])

            def all_pairs(n, values, into, op, empty, count):
                first = n == 0
                dmas = 48 * n + 48 * P * n
                c = count

                def link(ins, at):
                    ins.then_inc(all_step, 1)
                    pool.wait_ge(all_step, at)
                    pool.sem_inc(all_fence, 1)

                link(pool.memset(into, empty), c + 1)
                link(pool.memset(all_count, 0.0) if first else pool.memset(all_less, 0.0), c + 2)
                link(pool.iota(edge_no, pattern=[[1, TILES]], base=0, channel_multiplier=TILES,
                               allow_small_or_imprecise_dtypes=True) if first else pool.memset(all_less, 0.0), c + 3)
                c += 3
                pool.dma_start(scr_rows[:, 0:HEADS, :], heads(values)).then_inc(all_dma, 16)
                pool.dma_start(scr_rows[:, HEADS, :], dst_f[:, :]).then_inc(all_dma, 16)
                pool.dma_start(scr_rows[:, HEADS + 1, :], edge_no).then_inc(all_dma, 16)
                pool.wait_ge(all_dma, dmas + 48)
                dmas += 48
                steps_of = (8 if op == ALU.max else 4) + (4 if first else 0)
                with pool.Fori(0, P) as q:
                    pool.dma_start(heads(all_row), scr_rows[bass.ds(q, 1), 0:HEADS, :]
                                   .to_broadcast([P, HEADS, TILES])).then_inc(all_dma, 16)
                    pool.dma_start(all_dst, scr_rows[bass.ds(q, 1), HEADS, :].to_broadcast([P, TILES]))\
                        .then_inc(all_dma, 16)
                    pool.dma_start(all_idx, scr_rows[bass.ds(q, 1), HEADS + 1, :].to_broadcast([P, TILES]))\
                        .then_inc(all_dma, 16)
                    pool.wait_ge(all_dma, q * 48 + (dmas + 48))
                    pool.sem_inc(all_fence, 1)
                    with pool.Fori(0, TILES) as t:
                        at = [q * (TILES * steps_of) + t * steps_of + c]

                        def one(ins):
                            at[0] = at[0] + 1
                            link(ins, at[0])

                        one(pool.tensor_copy(all_col[:, 0:1], all_dst[:, bass.ds(t, 1)]))
                        one(pool.tensor_scalar(all_mask, dst_f[:, :], all_col[:, 0:1], None, ALU.is_equal))
                        if first:
                            one(pool.tensor_copy(all_col[:, 1:2], all_idx[:, bass.ds(t, 1)]))
                            one(pool.tensor_scalar(all_less, edge_no, all_col[:, 1:2], None, ALU.is_gt))
                            one(pool.tensor_tensor(all_less, all_less, all_mask, ALU.mult))
                            one(pool.tensor_tensor(all_count, all_count, all_less, ALU.add))
                        mask_b = all_mask[:, None, :].to_broadcast([P, HEADS, TILES])
                        value_b = heads(all_row)[:, :, bass.ds(t, 1)].to_broadcast([P, HEADS, TILES])
                        if op == ALU.max:
                            one(pool.tensor_copy(all_col[:, 2:2 + HEADS], heads(all_row)[:, :, bass.ds(t, 1)]
                                                 .rearrange("p h o -> p (h o)")))
                            for h in range(HEADS):
                                ins = pool.tensor_scalar(heads(all_prod)[:, h, :], heads(into)[:, h, :],
                                                         all_col[:, 2 + h:3 + h], None, ALU.max)
                            one(ins)
                            one(pool.tensor_tensor(heads(all_prod), heads(all_prod), mask_b, ALU.mult))
                            one(pool.tensor_scalar(all_mask, all_mask, -1.0, 1.0, ALU.mult, ALU.add))
                            one(pool.tensor_tensor(heads(into), heads(into), mask_b, ALU.mult))
                        else:
                            one(pool.tensor_tensor(heads(all_prod), mask_b, value_b, ALU.mult))
                        one(pool.tensor_tensor(into, into, all_prod, ALU.add))
                c += P * TILES * steps_of
                if first:
                    link(pool.tensor_scalar(rep_f[:, :], all_count, 0.0, None, ALU.is_equal), c + 1)
                    link(pool.tensor_scalar(scat_f[:, :], dst_f[:, :], NO_ROW, None, ALU.subtract), c + 2)
                    link(pool.tensor_tensor(scat_f[:, :], scat_f[:, :], rep_f[:, :], ALU.mult), c + 3)
                    link(pool.tensor_scalar(scat_f[:, :], scat_f[:, :], NO_ROW, None, ALU.add), c + 4)
                    link(pool.tensor_copy(scat_i[:, :], scat_f[:, :]), c + 5)
                    c += 5
                return c

            c = 0
            for n, (op, empty) in enumerate([(ALU.max, -BIG), (ALU.add, 0.0)]):
                pool.wait_ge(fast_done, n + 1)
                with pool.If(is_unsorted):
                    for s in range(2):
                        pool.wait_ge(out_stored[s], CHUNKS // 2 * 16)
                    c = all_pairs(n, scores[:, :, :].rearrange("p h t -> p (h t)"), total, op, empty, c)
                pool.sem_inc(reduced, 1)

            def stage_scat(g, j):
                pool.tensor_copy(scat_stage[:, j, :], scat_i[:, bass.ds(g * G, G)]).then_inc(scat_staged, 1)

            for s in range(2):
                pool.wait_ge(out_stored[s], CHUNKS // 2 * 16)
            stage_scat(0, 0)

            def scatter(g, k, j):
                pool.wait_ge(scat_staged, g + 1)
                pool.wait_ge(rows_ready, g + 1)
                if there(g + 1, GROUPS):
                    after(pool, scattered[(j + 1) % UNROLL], (k if j < 3 else k + 1) * (16 * G))
                    stage_scat(g + 1, (j + 1) % UNROLL)
                for t in range(G):
                    pool.indirect_dma_start(out, bass.IndirectOffsetOnAxis(ap=scat_stage[:, j, t:t + 1], axis=0),
                                            rows_out[:, j, t * D:(t + 1) * D], None,
                                            bounds_check=N_NODES - 1, oob_is_err=False)\
                        .then_inc(scattered[j], 16)

            steps(pool, scatter, GROUPS, GROUPS // UNROLL)
            for j in range(UNROLL):
                pool.wait_ge(scattered[j], len(range(j, GROUPS, UNROLL)) * 16 * G)

        @block.scalar
        def _(act):
            act.dma_start(consts[:, :], a["consts"]).then_inc(consts_loaded, 16)
            act.dma_start(bias_b, a["biases"].rearrange("p (n d) -> p n d", n=3)).then_inc(consts_loaded, 16)
            act.wait_ge(consts_loaded, 32)
            act.wait_ge(ident_made, 7)
            act.activation(tmp[:, 0, 4, 1, 0:1], eps[:, 0:1], ACT.Sqrt)

            def normalise(dst, src, norm, w, rows, done):
                for r in range(rows):
                    last = act.activation(dst[0:w, r * D:(r + 1) * D], src[0:w, r * D:(r + 1) * D], ACT.Identity,
                                          scale=norm[0:w, 0, r:r + 1], bias=norm[0:w, 1, r:r + 1])
                last.then_inc(done, 1)

            def deviation(q, which, rows, c):
                act.wait_ge(var_ready, c + 1)
                act.activation(tmp[:, q, 4, which, 0:rows], tmp[:, q, 3, which, 0:rows], ACT.Sqrt,
                               bias=eps[:, 0:1]).then_inc(std_ready, 1)

            def step(i, k, j):
                g = half(k, j)
                which = joint(i, CHUNKS, 2)
                if there(i - 1, CHUNKS + 2):
                    act.wait_ge(norm_ready, i)
                if there(i - 3, CHUNKS):
                    q = (j - 3) % 2
                    after(act, out_stored[q], (half(k, 0) + (j - 3) // 2) * 16)
                    for c in range(2):
                        normalise(o[:, q, c * 512:(c + 1) * 512], z_ps[q][:, c, :],
                                  norm2[:, q, :, c * G:(c + 1) * G], width(i - 3), G, out_ready)
                if there(i - 1, CHUNKS):
                    q = (j - 1) % UNROLL
                    for first, end in ((DVE_ROWS[q % 2], G), (G, ROWS)):
                        normalise(y[:, q, first * D:end * D], y[:, q, first * D:end * D],
                                  norm1[:, q % 2, :, first:end], width(i - 1), end - first, u_ready)
                if which:
                    deviation(j % 2, which, ROWS, i)
                if j % 2 == 0 and there(g, GROUPS):
                    act.wait_ge(turned, g + 1)
                    act.activation(xdT[:, bass.ds(g * GE, GE)], bank_xd, ACT.Copy)
                    act.activation(xsT[:, :], bank_xs, ACT.Copy)
                    act.activation(cdT[:, :], bank_ea[0:G, 2 * P:4 * P], ACT.Copy)
                    after(act, parts_ps, g)
                    act.activation(eaT[:, :], bank_ea[:, 0:2 * P], ACT.Copy).then_inc(turned_kept, 1)
                if j % 2 == 1 and there(g, GROUPS):
                    act.wait_ge(qk_ready, g + 1)
                    act.activation(qT[:, :], bank_xs, ACT.Identity, bias=bq[:, 0:1]).then_inc(q_kept, 1)
                    act.wait_ge(hidden_ps, g + 1)
                    act.activation(h1[:, :], bank_ea[:, 0:P], ACT.Relu, bias=bc1[:, 0:1])
                    act.activation(h2[:, :], bank_ea[0:G * DIST_H, P:2 * P], ACT.Relu, bias=bd1[:, 0:1])\
                        .then_inc(hidden_kept, 1)

            steps(act, step, CHUNKS + 1, CHUNKS // UNROLL - 1)
            act.wait_ge(scores_ready, 3 * GROUPS)
            act.activation(cons_all[:, :, :], cons_all[:, :, :], ACT.Sigmoid).then_inc(sig_ready, 1)
            for i in range(CHUNKS + 1, CHUNKS + 3):
                step(i, i // UNROLL, i % UNROLL)

            act.wait_ge(shifted, 1)
            flat = scores[:, :, :].rearrange("p h t -> p (h t)")
            act.activation(flat, flat, ACT.Exp).then_inc(exp_ready, 1)

            def step2(s, k, j):
                q = j % 2
                which = joint(s - 3, GROUPS, 2)
                if there(s - 2, GROUPS):
                    act.wait_ge(agg_turned, s - 1)
                    after(act, y2_ready, s - 3)
                    act.activation(aggT[:, q, :], T_ps[q], ACT.Copy).then_inc(aggT_ready, 1)
                if there(s - 6, GROUPS):
                    act.wait_ge(norm_ready, s + JOINT2)
                    row = rows_out[:, (j - 6) % UNROLL, :]
                    normalise(row, row, norm2[:, 1 - q, :, :], P, G, rows_ready)
                if which:
                    deviation(q, which, G, s + JOINT2)
                if there(s, GROUPS):
                    if isinstance(s, int) and s == XG_EARLY:
                        act.wait_ge(S_ready, 1)
                    after(act, xb_ready, s - 7)
                    act.activation(xg[:, j, :], xdT[:, bass.ds(s * GE, GE)], ACT.Copy).then_inc(xg_ready, 1)
                if there(s - 3, GROUPS):
                    act.wait_ge(norm_ready, s + JOINT2 + 1)
                    normalise(u[:, 1 - q, :], Y_ps[1 - q], norm1[:, q, :, :], P, G, u2_ready)

            steps(act, step2, GROUPS + 6, GROUPS // SLOTS2, 1, SLOTS2)

        @block.vector
        def _(dve):
            done = [0]

            def link(ins, s=setup_step):
                done[0] += 1
                ins.then_inc(s, 1)
                dve.wait_ge(s, done[0])

            dve.wait_ge(idx_loaded, 64)
            dve.tensor_copy(dst_f[:, :], dst_i)
            link(dve.tensor_copy(prev_f[:, :], prev_i[:, :]))
            dve.tensor_tensor(unsorted_t[:, :], prev_f[:, :], dst_f[:, :], ALU.is_gt)
            dve.tensor_tensor(same[:, :], prev_f[:, :], dst_f[:, :], ALU.is_equal)
            dve.tensor_scalar(in_first[:, :], dst_f[:, :], dst_f[:, 0:1], None, ALU.is_equal)
            link(dve.tensor_scalar(in_last[:, :], dst_f[:, :], dst_f[:, TILES - 1:TILES], None, ALU.is_equal))
            dve.tensor_reduce(unsorted_p[:, :], unsorted_t[:, :], AX.X, ALU.add)
            dve.tensor_scalar(neg_first[:, :], in_first[:, :], -1.0, BIG, ALU.add, ALU.mult)
            dve.tensor_scalar(neg_last[:, :], in_last[:, :], -1.0, BIG, ALU.add, ALU.mult)
            same_b = same[:, None, :].to_broadcast([P, HEADS, TILES])
            dve.tensor_copy(heads(cont_f)[:, :, 1:TILES], same_b[:, :, 1:TILES])
            dve.memset(heads(cont_f)[:, :, 0:1], 0.0)
            dve.memset(cont[:, HT:HT + 1], 0.0)
            dve.tensor_copy(link8[:, 0, :], same[:, 0:1].to_broadcast([P, HEADS]))
            dve.tensor_copy(link8[:, 1, :], in_first[:, TILES - 1:TILES].to_broadcast([P, HEADS]))
            link(dve.tensor_scalar(rep_f[:, :], same[:, :], -1.0, 1.0, ALU.mult, ALU.add))
            link(dve.scalar_tensor_tensor(scat_f[:, :], dst_f[:, :], -NO_ROW, rep_f[:, :], ALU.add, ALU.mult))
            link(dve.tensor_scalar(scat_f[:, :], scat_f[:, :], NO_ROW, None, ALU.add))
            link(dve.tensor_copy(scat_i[:, :], scat_f[:, :]))
            dve.memset(mul_r[:, :, :], 0.0).then_inc(masks_made_pe, 1)

            dve.wait_ge(consts_loaded, 32)
            dve.wait_ge(ident_made, 7)
            link(dve.tensor_copy(part_bf[:, 0], bias_b))
            link(dve.tensor_tensor(part_f[:, 0], bias_b, part_bf[:, 0], ALU.subtract))
            link(dve.tensor_copy(part_bf[:, 1], part_f[:, 0]))
            link(dve.tensor_tensor(part_f[:, 1], part_f[:, 0], part_bf[:, 1], ALU.subtract))
            link(dve.tensor_copy(part_bf[:, 2], part_f[:, 1]))
            link(dve.tensor_scalar(part_f[:, 0], part_bf[:, 0], ident[:, 0:1], None, ALU.mult))
            link(dve.scalar_tensor_tensor(part_f[:, 1], part_bf[:, 1], ident[:, 1:2], part_f[:, 0],
                                          ALU.mult, ALU.add))
            link(dve.scalar_tensor_tensor(part_f[:, 0], part_bf[:, 2], ident[:, 2:3], part_f[:, 1],
                                          ALU.mult, ALU.add))
            dve.tensor_copy(bias_rows[:, :, :], part_f[:, 0]).then_inc(bias_split, 1)

            dve.wait_ge(links_turned, 1)
            dve.tensor_copy(unsorted_i[:, :], bank_sc[:, 256:257]).then_inc(masks_made, 1)
            link(dve.tensor_copy(link_r[:, :, :], bank_sc[0:HEADS, 0:256].rearrange("p (a b) -> p a b", a=2)))
            linked, whole = link_r[:, 0, :], link_r[:, 1, :]
            dve.tensor_tensor(mul_r[:, 0, 1:P], linked[:, 1:P], whole[:, 0:P - 1], ALU.mult)
            dve.tensor_tensor(mul_r[:, 1, 0:P - 1], linked[:, 1:P], whole[:, 1:P], ALU.mult)
            dve.tensor_copy(mul_r[:, 2, 1:P], linked[:, 1:P])
            link(dve.tensor_copy(mul_r[:, 3, 0:P - 1], linked[:, 1:P]))
            link(dve.tensor_scalar(neg_r[:, :, :], mul_r[:, :, :], -1.0, BIG, ALU.add, ALU.mult))

            def variances(q, which, rows, c, last, between):
                last.then_inc(stat, 1)
                between[0]()
                dve.wait_ge(stat, c * 3 + 1)
                even, odd = st[:, q, which, 0:rows, 1:3], st[:, q, which, 0:rows, 4:6]
                two_mean, sq, diff, var = (tmp[:, q, n, which, 0:rows] for n in range(4))
                dve.tensor_tensor(diff, even[:, :, :, 0], odd[:, :, :, 0], ALU.subtract)
                dve.tensor_tensor(tmp[:, q, 0:2, which, 0:rows].rearrange("p n w r -> p w r n"), even, odd, ALU.add)\
                   .then_inc(stat, 1)
                between[1]()
                dve.wait_ge(stat, c * 3 + 2)
                dve.scalar_tensor_tensor(diff, diff, 0.25, diff, ALU.mult, ALU.mult).then_inc(stat, 1)
                between[2]()
                dve.wait_ge(stat, c * 3 + 3)
                dve.scalar_tensor_tensor(var, sq, 1.0 / D, diff, ALU.mult, ALU.add).then_inc(var_ready, 1)

            def factors(q, which, rows, c, between):
                dve.wait_ge(std_ready, c + 1)
                inv, shift = norm[:, q, 0, which, 0:rows], norm[:, q, 1, which, 0:rows]
                dve.reciprocal(inv, tmp[:, q, 4, which, 0:rows]).then_inc(inv_ready, 1)
                between()
                dve.wait_ge(inv_ready, c + 1)
                dve.scalar_tensor_tensor(shift, tmp[:, q, 0, which, 0:rows], -0.5, inv, ALU.mult, ALU.mult)\
                   .then_inc(norm_ready, 1)

            def nothing():
                pass

            def times_gamma(buf, w, rows, done_sem):
                v = buf[0:w, :].rearrange("p (r d) -> p r d", d=D)
                dve.tensor_tensor(v, v, gamma_b[0:w, None, :].to_broadcast([w, rows, D]), ALU.mult)\
                   .then_inc(done_sem, 1)

            def rows_before(k, j):
                return k * (UNROLL // 2 * sum(DVE_ROWS)) + sum(DVE_ROWS[n % 2] for n in range(j))

            def combine_scores():
                done[0] = 0
                link(dve.tensor_scalar(neg, cont[:, :], -1.0, BIG, ALU.add, ALU.mult), soft_step)
                dve.wait_ge(sig_ready, 1)
                link(dve.tensor_tensor(scores[:, :, :], scores[:, :, :], cons_all[:, :, :], ALU.mult), soft_step)
                link(dve.tensor_tensor(scores[:, :, :], scores[:, :, :], dist_all[:, :, :], ALU.add), soft_step)

            def step(i, k, j):
                g = half(k, j)
                q = j % 2
                which = joint(i, CHUNKS, 2)
                if there(i, CHUNKS):
                    w = width(i)
                    dve.wait_ge(x_loaded[j], k * 16 + 16)
                    dve.tensor_tensor(
                        y[0:w, j, POOL_ROWS * D:].rearrange("p (r d) -> p r d", d=D),
                        x_in[0:w, j, POOL_ROWS * D:].rearrange("p (r d) -> p r d", d=D),
                        bo_b[0:w, None, :].to_broadcast([w, ROWS - POOL_ROWS, D]), ALU.add).then_inc(own_y, 1)
                    dve.wait_ge(y_ready, i + 1)
                    for r in range(ROWS):
                        if r == POOL_ROWS:
                            dve.wait_ge(own_y, i + 1)
                        last = dve.bn_stats(st[0:w, q, 0, r, :], y[0:w, j, r * D:(r + 1) * D])
                if there(i - 2, CHUNKS):
                    w = width(i - 2)
                    for r in range(ROWS):
                        if r % G == 0:
                            dve.wait_ge(z_ready, (i - 2) * 2 + r // G + 1)
                        last = dve.bn_stats(st[0:w, q, 1, r, :], z_ps[q][0:w, r // G, r % G * D:(r % G + 1) * D])

                def own_row(r):
                    if there(i - 1, CHUNKS) and r < DVE_ROWS[1 - q]:
                        if r == 0:
                            dve.wait_ge(norm_ready, i)
                        w = width(i - 1)
                        row = y[0:w, (j - 1) % UNROLL, r * D:(r + 1) * D]
                        dve.tensor_scalar(row, row, norm1[0:w, 1 - q, 0, r:r + 1], norm1[0:w, 1 - q, 1, r:r + 1],
                                          ALU.mult, ALU.add).then_inc(rows_normed, 1)

                def own_rest():
                    for r in range(1, max(DVE_ROWS)):
                        own_row(r)

                def scale(c):
                    if there(i - 1, CHUNKS):
                        if c == 0:
                            dve.wait_ge(rows_normed, rows_before(k, j))
                        dve.wait_ge(u_ready, 2 * i - 1 + c)
                        times_gamma(y[:, (j - 1) % UNROLL, c * 512:(c + 1) * 512], width(i - 1), G, ug_ready)

                def edge_part(n):
                    if j % 2 == 0 and there(g - 1, GROUPS):
                        if n == 0:
                            dve.wait_ge(parts_ps, g)
                        into, bias = ((scores, be_b), (cons_all, bc2_b), (dist_all, bd2_b))[n]
                        dve.tensor_tensor(
                            into[:, :, bass.ds(g * G - G, G)],
                            bank_sc[:, n * G * HEADS:(n + 1) * G * HEADS].rearrange("p (t h) -> p h t", h=HEADS),
                            bias[:, :, None].to_broadcast([P, HEADS, G]), ALU.add).then_inc(scores_ready, 1)

                if which:
                    variances(q, which, ROWS, i, last, (lambda: own_row(0), own_rest,
                                                        lambda: edge_part(0)))
                    edge_part(1)
                    scale(0)
                    if isinstance(i, int) and i == CHUNKS + 1:
                        combine_scores()
                    factors(q, which, ROWS, i, lambda: edge_part(2))
                    scale(1)
                if j % 2 == 1 and there(g, GROUPS):
                    dve.wait_ge(q_kept, g + 1)
                    dve.scalar_tensor_tensor(prod[:, :], bank_xd, bk[:, 0:1], qT[:, :], ALU.add, ALU.mult)\
                       .then_inc(prod_ready, 1)

            steps(dve, step, CHUNKS + 2, CHUNKS // UNROLL - 1)

            flat = scores[:, :, :].rearrange("p h t -> p (h t)")

            def soft(ins):
                link(ins, soft_step)

            def segments(n, masks, op0, op, start, masks_r, comb0, in_masks):
                soft(dve.tensor_tensor_scan(run, masks[0], flat, start, op0, op))
                soft(dve.tensor_tensor_scan(total[:, ::-1], masks[1][:, ::-1], run[:, ::-1], 0.0, op0, ALU.max))
                dve.sem_inc(edges_out, 1)
                dve.wait_ge(edges_turned, n + 1)
                first_r, last_r = bank_sc[0:HEADS, 0:P], bank_sc[0:HEADS, P:2 * P]
                dve.tensor_tensor(edge_r[:, 0, 1:P], last_r[:, 0:P - 1], masks_r[:, 2, 1:P], comb0)
                dve.tensor_tensor(edge_r[:, 1, 0:P - 1], first_r[:, 1:P], masks_r[:, 3, 0:P - 1], comb0)
                dve.memset(edge_r[:, 0, 0:1], start)
                soft(dve.memset(edge_r[:, 1, P - 1:P], start))
                dve.tensor_tensor_scan(carry_r[:, 0, :], masks_r[:, 0, :], edge_r[:, 0, :], start, op0, op)
                dve.tensor_tensor_scan(carry_r[:, 1, ::-1], masks_r[:, 1, ::-1], edge_r[:, 1, ::-1], start, op0, op)\
                   .then_inc(carries_out, 1)
                dve.wait_ge(carries_turned, n + 1)
                soft(dve.tensor_copy(carry[:, :, :], bank_sc[:, 256:256 + 2 * HEADS]
                                     .rearrange("p (a b) -> p a b", a=2)))
                th = heads(total)
                for side in range(2):
                    for h in range(HEADS):
                        last = dve.scalar_tensor_tensor(th[:, h, :], in_masks[side][:, :], carry[:, side, h:h + 1],
                                                        th[:, h, :], comb0, op)
                    soft(last)
                dve.sem_inc(fast_done, 1)
                dve.wait_ge(reduced, n + 1)

            segments(0, (neg_f, neg_b), ALU.add, ALU.max, -BIG, neg_r, ALU.add, (neg_first, neg_last))
            dve.tensor_tensor(flat, flat, total, ALU.subtract).then_inc(shifted, 1)
            dve.wait_ge(exp_ready, 1)
            segments(1, (cont_f, cont_b), ALU.mult, ALU.add, 0.0, mul_r, ALU.mult, (in_first, in_last))

            def shares(part):
                cols = slice(S_PARTS[part] * G, S_PARTS[part + 1] * G)
                soft(dve.reciprocal(dist_all[:, :, cols], th_all[:, :, cols]))
                soft(dve.tensor_tensor(scores[:, :, cols], th_all[:, :, cols], dist_all[:, :, cols], ALU.mult))

            shares(0)
            dve.sem_inc(S_ready, 1)

            def step2(s, k, j):
                q = j % 2
                which = joint(s - 3, GROUPS, 2)
                slot = (j - 4) % UNROLL
                if there(s - 3, GROUPS):
                    dve.wait_ge(y2_ready, s - 2)
                    for r in range(G):
                        last = dve.bn_stats(st[:, q, 0, r, :], Y_ps[1 - q][:, r * D:(r + 1) * D])
                if there(s - 5, GROUPS):
                    dve.wait_ge(z2_ready, s - 4)
                    for r in range(G):
                        last = dve.bn_stats(st[:, q, 1, r, :], rows_out[:, (slot - 1) % UNROLL, r * D:(r + 1) * D])

                def scale():
                    if there(s - 4, GROUPS):
                        dve.wait_ge(u2_ready, s - 3)
                        times_gamma(u[:, q, :], P, G, ug2_ready)

                def add_x():
                    if there(s - 4, GROUPS):
                        if isinstance(s, int) and s == 4:
                            for n in range(2):
                                dve.wait_ge(out_stored[n], CHUNKS // 2 * 16)
                        after(dve, scattered[slot], (k * 2 + (j - 4) // UNROLL) * (16 * G))
                        dve.wait_ge(ug2_ready, s - 3)
                        dve.wait_ge(xb_ready, s - 3)
                        dve.tensor_tensor(rows_out[:, slot, :], u[:, q, :], XB_ps[q], ALU.add).then_inc(z2_ready, 1)

                def weigh():
                    if there(s - 1, GROUPS):
                        dve.wait_ge(v_ready, s)
                        after(dve, agg_turned, s - 2)
                        S = scores[:, :, bass.ds((s - 1) * G, G)].rearrange("p h t -> p t h")
                        dve.tensor_tensor(agg[:, 1 - q, :].rearrange("p (t h d) -> p t h d", t=G, h=HEADS),
                                          V_ps[1 - q].rearrange("p (t h d) -> p t h d", t=G, h=HEADS),
                                          S[:, :, :, None].to_broadcast([P, G, HEADS, HEAD_DIM]), ALU.mult)\
                           .then_inc(agg_ready, 1)

                if which:
                    variances(q, which, G, s + JOINT2, last, (scale, weigh, nothing))
                    add_x()
                else:
                    weigh()
                if which:
                    factors(q, which, G, s + JOINT2, nothing)
                if isinstance(s, int) and 1 <= s < len(S_PARTS) - 1:
                    shares(s)

            steps(dve, step2, GROUPS + 5, GROUPS // SLOTS2, 1, SLOTS2)

        @block.tensor
        def _(pe):
            pe.wait_ge(ident_made, 7)
            pe.wait_ge(masks_made_pe, 1)
            pe.transpose(bank_sc[0:HEADS, 0:P], link8[:, 0, :], ident[:, :])
            pe.transpose(bank_sc[0:HEADS, P:2 * P], link8[:, 1, :], ident[:, :])
            pe.matmul(bank_sc[:, 256:257], ones[:, :], unsorted_p[:, :], start=True, stop=True)\
              .then_inc(links_turned, 1)
            pe.wait_ge(consts_loaded, 32)
            pe.wait_ge(bias_split, 1)
            pe.wait_ge(masks_made, 1)

            def by_tile(bank):
                return bank.rearrange("p (t d) -> p t d", d=D)

            def dense_x(i, j):
                w = width(i)
                for c in range(2):
                    after(pe, out_ready, 2 * i - 3 + c)
                    pe.matmul(by_tile(z_ps[j % 2][0:w, c, :]), ones_bf[:, 0:w], beta_rows,
                              start=True, stop=False)
                    last = pe.matmul(z_ps[j % 2][0:w, c, :], ident[0:w, 0:w], x_in[0:w, j, c * 512:(c + 1) * 512],
                                     start=False, stop=False)
                last.then_inc(x_used, 1)

            def dense_z(i, j):
                w = width(i)
                for c in range(2):
                    pe.wait_ge(ug_ready, 2 * i + c + 1)
                    pe.matmul(z_ps[j % 2][0:w, c, :], ident[0:w, 0:w], y[0:w, j, c * 512:(c + 1) * 512],
                              start=False, stop=True).then_inc(z_ready, 1)

            def step(i, k, j):
                g = half(k, j)
                s = j // 2
                if j % 2 == 0 and there(g - 1, GROUPS):
                    pe.wait_ge(prod_ready, g)
                    pe.wait_ge(hidden_kept, g)
                    after(pe, scores_ready, 3 * g - 3)
                    for t in range(2):
                        pe.matmul(bank_sc[:, t * 2 * HEADS:(t + 1) * 2 * HEADS], eaT[:, t * P:(t + 1) * P], We2[:, :],
                                  start=True, stop=False)
                        for c in range(2):
                            pe.matmul(bank_sc[:, t * 2 * HEADS:(t + 1) * 2 * HEADS],
                                      prod[:, (2 * t + c) * P:(2 * t + c + 1) * P],
                                      head_sel3[:, (1 - c) * HEADS:(3 - c) * HEADS], start=False, stop=c == 1)
                    pe.matmul(bank_sc[:, G * HEADS:2 * G * HEADS], h1[:, :], Wc2s[:, :], start=True, stop=True)
                    pe.matmul(bank_sc[:, 2 * G * HEADS:3 * G * HEADS], h2[:, :], Wd2s[:, :], start=True, stop=True)\
                      .then_inc(parts_ps, 1)
                if j % 2 == 0 and there(g, GROUPS):
                    pe.wait_ge(gathered[s], (k + 1) * (16 * 2 * G))
                    pe.wait_ge(ea_loaded[s], (k + 1) * 16)
                    pe.wait_ge(dist_staged, g + 1)
                    after(pe, q_kept, g)
                    after(pe, prod_ready, g)
                    after(pe, hidden_kept, g)
                    for t in range(G):
                        pe.transpose(bank_xd[:, t * P:(t + 1) * P], xd[:, s, t, 0:D], ident[:, :])
                    for t in range(G):
                        pe.transpose(bank_xs[:, t * P:(t + 1) * P], xs[:, s, t, :], ident[:, :])
                    for t in range(2):
                        pe.transpose(bank_ea[:, t * P:(t + 1) * P], ea[:, s, t * P:(t + 1) * P], ident[:, :])
                    pe.transpose(bank_ea[0:G, 2 * P:3 * P], xd[:, s, :, D], ident[:, :])
                    pe.transpose(bank_ea[0:G, 3 * P:4 * P], dist_s[:, s, :], ident[:, :])\
                      .then_inc(turned, 1)
                if j % 2 == 1 and there(g, GROUPS):
                    pe.wait_ge(turned_kept, g + 1)
                    pe.matmul(bank_xs, Wq[:, :], xsT[:, :], start=True, stop=True)
                    pe.matmul(bank_xd, Wk[:, :], xdT[:, bass.ds(g * GE, GE)], start=True, stop=True)\
                      .then_inc(qk_ready, 1)
                    pe.matmul(bank_ea[:, 0:P], Wc1s[:, :], cdT[:, 0:P], start=True, stop=True)
                    pe.matmul(bank_ea[0:G * DIST_H, P:2 * P], Wd1s[:, :], cdT[:, P:2 * P], start=True, stop=True)\
                      .then_inc(hidden_ps, 1)
                if there(i - 1, CHUNKS):
                    dense_x(i - 1, (j - 1) % UNROLL)
                    dense_z(i - 1, (j - 1) % UNROLL)

            steps(pe, step, CHUNKS + 1, CHUNKS // UNROLL - 1)

            th = heads(total)
            for n in range(2):
                pe.wait_ge(edges_out, n + 1)
                pe.transpose(bank_sc[0:HEADS, 0:P], th[:, :, 0], ident[:, :])
                pe.transpose(bank_sc[0:HEADS, P:2 * P], th[:, :, TILES - 1], ident[:, :]).then_inc(edges_turned, 1)
                pe.wait_ge(carries_out, n + 1)
                for side in range(2):
                    last = pe.transpose(bank_sc[:, 256 + side * HEADS:256 + (side + 1) * HEADS], carry_r[:, side, :],
                                        ident[0:HEADS, 0:HEADS])
                last.then_inc(carries_turned, 1)

            def add_bias(into, rows):
                return pe.matmul(by_tile(into), ones_bf[:, :], rows, start=False, stop=True, skip_group_check=True)

            def product(into, turned_rows, weights, first, turn=False):
                for t in range(G):
                    pe.matmul(into[:, t * P:(t + 1) * P], turned_rows[:, t * P:(t + 1) * P], weights,
                              start=first and t == 0, stop=False, is_transpose=turn, skip_group_check=True)

            def step2(s, k, j):
                q = j % 2
                if there(s - 2, GROUPS):
                    pe.wait_ge(agg_ready, s - 1)
                    after(pe, aggT_ready, s - 3)
                    for t in range(G):
                        last = pe.transpose(T_ps[q][:, t * P:(t + 1) * P], agg[:, q, t * P:(t + 1) * P], ident[:, :])
                    last.then_inc(agg_turned, 1)
                if there(s - 1, GROUPS):
                    pe.wait_ge(xg_ready, s)
                    after(pe, agg_ready, s - 2)
                    product(V_ps[1 - q], xg[:, (j - 1) % SLOTS2, :], Wv[:, :], True)
                    add_bias(V_ps[1 - q], bv_rows).then_inc(v_ready, 1)
                if there(s - 3, GROUPS):
                    after(pe, z2_ready, s - 4)
                    product(XB_ps[1 - q], xg[:, (j - 3) % SLOTS2, :], ident[:, :], True, turn=True)
                    add_bias(XB_ps[1 - q], beta_rows).then_inc(xb_ready, 1)
                if there(s - 2, GROUPS):
                    pe.wait_ge(aggT_ready, s - 1)
                    after(pe, u2_ready, s - 3)
                    product(Y_ps[q], xg[:, (j - 2) % SLOTS2, :], ident[:, :], True, turn=True)
                    product(Y_ps[q], aggT[:, q, :], Wo[:, :], False)
                    add_bias(Y_ps[q], bo_rows).then_inc(y2_ready, 1)

            steps(pe, step2, GROUPS + 3, GROUPS // SLOTS2, 1, SLOTS2)


def kernel(**inputs):
    import numpy as _np
    import concourse.bacc as _bacc
    from concourse import mybir as _mybir
    from concourse.bass_utils import run_bass_kernel_spmd as _run

    nc = _bacc.Bacc("TRN2", target_bir_lowering=False, num_devices=1)
    pad = PAD_EDGES - N_EDGES

    def padded(v, fill):
        tail = _np.full((pad,) + v.shape[1:], fill, v.dtype)
        return _np.concatenate([v, tail])

    x = _np.asarray(inputs["x"])
    xn = _np.concatenate([x, _np.asarray(inputs["node_vec1"])], axis=1)
    xn = _np.concatenate([xn, _np.zeros((1, XN), x.dtype)])
    data = {
        "x": x, "xn": xn,
        "src": padded(_np.asarray(inputs["src"]), 0),
        "dst": _np.concatenate([_np.full(1, -1, _np.int32), padded(_np.asarray(inputs["dst"]), N_NODES)]),
        "edge_attr": padded(_np.asarray(inputs["edge_attr_64"]), 0),
        "edge_weight": padded(_np.asarray(inputs["edge_weight1"]).reshape(-1), 0),
    }
    w = {name[len("L0_gnn_"):]: _np.asarray(v) for name, v in inputs.items() if name.startswith("L0_gnn_")}

    def diagonal(v, n):
        r, c = v.shape
        block = _np.zeros((n * r, n * c), v.dtype)
        for i in range(n):
            block[i * r:(i + 1) * r, i * c:(i + 1) * c] = v
        return block

    w.update(We2=diagonal(w["We"], 2), Wc1s=diagonal(w["Wc1"], G), Wd1s=diagonal(w["Wd1"], G),
             Wc2s=diagonal(w["Wc2"], G), Wd2s=diagonal(w["Wd2"], G),
             bc1s=_np.concatenate([w["bc1"]] * G), bd1s=_np.concatenate([w["bd1"]] * G))
    consts = _np.zeros((P, CONST_COLS), x.dtype)
    for name, (rows, cols, at) in CONSTS.items():
        v = w[name]
        consts[0:rows, at:at + cols] = v.reshape(rows, cols) if v.size == rows * cols else v.reshape(1, cols)
    data["consts"] = consts
    data["biases"] = _np.broadcast_to(_np.concatenate([w["beta"], w["bo"], w["bv"]]), (P, 3 * D))
    arrays, args = {}, {}
    for name, v in data.items():
        v = _np.ascontiguousarray(v)
        arrays[f"in_{name}_dram"] = v
        args[name] = nc.dram_tensor(f"in_{name}_dram", v.shape, _mybir.dt.from_np(v.dtype), kind="ExternalInput").ap()
    out = nc.dram_tensor("out_0_dram", (N_NODES, D), _mybir.dt.float32, kind="ExternalOutput").ap()
    gnn_kernel(nc, args, out)
    r = _run(nc, [arrays], core_ids=[0])
    return r.results[0]["out_0_dram"]
```
